# Optimizing a Trainium2 kernel written in Bass

```python
import numpy as np
import jax
import jax.numpy as jnp

def _softmax(x, axis=-1):
    return jax.nn.softmax(x, axis=axis)

def _gelu(x):
    return jax.nn.gelu(x, approximate=True)

def _silu(x):
    return jax.nn.silu(x)

def _sigmoid(x):
    return jax.nn.sigmoid(x)

def _layernorm(x, axis=-1, eps=1e-05):
    m = jnp.mean(x, axis=axis, keepdims=True)
    v = jnp.var(x, axis=axis, keepdims=True)
    return (x - m) / jnp.sqrt(v + eps)

def _scatter_add(tgt, idx, src, axis=0):
    return tgt.at[idx].add(src)

def _segment_sum(src, seg, n):
    return jax.ops.segment_sum(src, seg, n)
kernel_name = 'mk_macaron_d1_jaxref_r4_8deaf8'

def setup_inputs(seed: int=0):
    np.random.seed(seed)
    _w = jnp.asarray

    def _L0_attn_setup():
        import jax, jax.numpy as jnp
        import numpy as np
        D, D_OUTER, R_STRIDE, N_LAYERS = (256, 64, 4, 3)
        EPS_NORM = 1e-12
        EPS_RMS = 1e-06

        def _rms_norm(x, w):
            var = jnp.mean(x * x, axis=-1, keepdims=True)
            return x * jax.lax.rsqrt(var + EPS_RMS) * w

        def _l2_normalize(x):
            n = jnp.sqrt(jnp.sum(x * x, axis=-1, keepdims=True))
            return x / jnp.maximum(n, EPS_NORM)

        def _recurrence_layer(x, cw, cb, wr_w, wr_b, wi_w, wi_b, log_a, ow, nw):
            B, L, d = x.shape
            xp = jnp.pad(x, ((0, 0), (3, 0), (0, 0)))
            x_conv = cb + sum((xp[:, k:k + L, :] * cw[:, k] for k in range(4)))
            r_t = jax.nn.sigmoid(x_conv @ wr_w.T + wr_b)
            i_t = jax.nn.sigmoid(x_conv @ wi_w.T + wi_b)
            a_t = jnp.exp(8.0 * r_t * jax.nn.log_sigmoid(log_a))
            inp = i_t * x_conv
            gate = jnp.sqrt(jnp.maximum(1.0 - a_t * a_t, 0.0))

            def step(h_prev, ts):
                a, g_inp = ts
                h = a * h_prev + g_inp
                return (h, h)
            a_T = jnp.swapaxes(a_t, 0, 1)
            gi_T = jnp.swapaxes(gate * inp, 0, 1)
            h0 = jnp.zeros((B, d), dtype=x.dtype)
            _, hs = jax.lax.scan(step, h0, (a_T, gi_T))
            out = jnp.swapaxes(hs, 0, 1)
            return _rms_norm(out @ ow.T, nw)

        def _reference_tuple_inner(h, down_w, up_w, conv_w, conv_b, Wr_w, Wr_b, Wi_w, Wi_b, log_a, out_w, norm_w):
            B, L, d = h.shape
            M = L // R_STRIDE
            x = h @ down_w.T
            for i in range(N_LAYERS):
                x = _recurrence_layer(x, conv_w[i], conv_b[i], Wr_w[i], Wr_b[i], Wi_w[i], Wi_b[i], log_a[i], out_w[i], norm_w[i])
            encoder_out = x @ up_w.T
            enc_n = _l2_normalize(encoder_out)
            sim = jnp.sum(enc_n[:, 1:] * enc_n[:, :-1], axis=-1)
            p = (1.0 - sim) * 0.5
            boundary_probs = jnp.pad(p, ((0, 0), (1, 0)), constant_values=1.0)
            _, topk_idx = jax.lax.top_k(boundary_probs, M)
            boundary_idx = jnp.sort(topk_idx, axis=1)
            concept_tokens = jnp.take_along_axis(encoder_out, boundary_idx[..., None], axis=1)
            return (concept_tokens, encoder_out, boundary_probs, boundary_probs, boundary_idx)
        key = jax.random.key(seed)
        ks = jax.random.split(key, 12)
        d, do = (D, D_OUTER)
        inp = {'h': jax.random.normal(ks[0], (4, 1024, d), dtype=jnp.float32), 'down_w': jax.random.normal(ks[1], (do, d), dtype=jnp.float32) * 0.02, 'up_w': jax.random.normal(ks[2], (d, do), dtype=jnp.float32) * 0.02, 'conv_w': jax.random.normal(ks[3], (N_LAYERS, do, 4), dtype=jnp.float32) * 0.02, 'conv_b': jnp.zeros((N_LAYERS, do), dtype=jnp.float32), 'Wr_w': jax.random.normal(ks[4], (N_LAYERS, do, do), dtype=jnp.float32) * 0.02, 'Wr_b': jnp.zeros((N_LAYERS, do), dtype=jnp.float32), 'Wi_w': jax.random.normal(ks[5], (N_LAYERS, do, do), dtype=jnp.float32) * 0.02, 'Wi_b': jnp.zeros((N_LAYERS, do), dtype=jnp.float32), 'log_a': jnp.full((N_LAYERS, do), 7.5, dtype=jnp.float32), 'out_w': jax.random.normal(ks[6], (N_LAYERS, do, do), dtype=jnp.float32) * 0.02, 'norm_w': jnp.ones((N_LAYERS, do), dtype=jnp.float32)}
        return inp
    _L0_attn_in = _L0_attn_setup()

    def _L0_ffn_setup():
        import jax, jax.numpy as jnp
        import numpy as np
        B, S, D, F, E = (4, 512, 256, 1024, 8)
        LN_EPS = 1e-05
        key = jax.random.key(seed)
        ks = jax.random.split(key, 6)
        sc = 0.02
        return {'x': jax.random.normal(ks[0], (B, S, D), dtype=jnp.float32), 'Wr': jax.random.normal(ks[1], (D, E), dtype=jnp.float32) * sc, 'br': jnp.zeros((E,), jnp.float32), 'ln_g': jnp.ones((D,), jnp.float32), 'ln_b': jnp.zeros((D,), jnp.float32), 'W1': jax.random.normal(ks[2], (E, D, F), dtype=jnp.float32) * sc, 'b1': jnp.zeros((E, F), jnp.float32), 'W2': jax.random.normal(ks[3], (E, F, D), dtype=jnp.float32) * sc, 'b2': jnp.zeros((E, D), jnp.float32)}
    _L0_ffn_in = _L0_ffn_setup()
    _d = {'L0_attn_h': _L0_attn_in['h'], 'L0_attn_down_w': _L0_attn_in['down_w'], 'L0_attn_up_w': _L0_attn_in['up_w'], 'L0_attn_conv_w': _L0_attn_in['conv_w'], 'L0_attn_conv_b': _L0_attn_in['conv_b'], 'L0_attn_Wr_w': _L0_attn_in['Wr_w'], 'L0_attn_Wr_b': _L0_attn_in['Wr_b'], 'L0_attn_Wi_w': _L0_attn_in['Wi_w'], 'L0_attn_Wi_b': _L0_attn_in['Wi_b'], 'L0_attn_log_a': _L0_attn_in['log_a'], 'L0_attn_out_w': _L0_attn_in['out_w'], 'L0_attn_norm_w': _L0_attn_in['norm_w'], 'L0_ffn_Wr': _L0_ffn_in['Wr'], 'L0_ffn_br': _L0_ffn_in['br'], 'L0_ffn_ln_g': _L0_ffn_in['ln_g'], 'L0_ffn_ln_b': _L0_ffn_in['ln_b'], 'L0_ffn_W1': _L0_ffn_in['W1'], 'L0_ffn_b1': _L0_ffn_in['b1'], 'L0_ffn_W2': _L0_ffn_in['W2'], 'L0_ffn_b2': _L0_ffn_in['b2']}
    _x0 = _d['L0_attn_h']
    _d['L0_attn_h'] = jax.random.normal(jax.random.fold_in(jax.random.key(seed), 1), (2, 2048, 256), dtype=_x0.dtype)
    del _x0
    return _d

def reference(L0_attn_h, L0_attn_down_w, L0_attn_up_w, L0_attn_conv_w, L0_attn_conv_b, L0_attn_Wr_w, L0_attn_Wr_b, L0_attn_Wi_w, L0_attn_Wi_b, L0_attn_log_a, L0_attn_out_w, L0_attn_norm_w, L0_ffn_Wr, L0_ffn_br, L0_ffn_ln_g, L0_ffn_ln_b, L0_ffn_W1, L0_ffn_b1, L0_ffn_W2, L0_ffn_b2):

    def _L0_attn_ref(h, down_w, up_w, conv_w, conv_b, Wr_w, Wr_b, Wi_w, Wi_b, log_a, out_w, norm_w):
        import jax, jax.numpy as jnp
        import numpy as np
        D, D_OUTER, R_STRIDE, N_LAYERS = (256, 64, 4, 3)
        EPS_NORM = 1e-12
        EPS_RMS = 1e-06

        def _rms_norm(x, w):
            var = jnp.mean(x * x, axis=-1, keepdims=True)
            return x * jax.lax.rsqrt(var + EPS_RMS) * w

        def _l2_normalize(x):
            n = jnp.sqrt(jnp.sum(x * x, axis=-1, keepdims=True))
            return x / jnp.maximum(n, EPS_NORM)

        def _recurrence_layer(x, cw, cb, wr_w, wr_b, wi_w, wi_b, log_a, ow, nw):
            B, L, d = x.shape
            xp = jnp.pad(x, ((0, 0), (3, 0), (0, 0)))
            x_conv = cb + sum((xp[:, k:k + L, :] * cw[:, k] for k in range(4)))
            r_t = jax.nn.sigmoid(x_conv @ wr_w.T + wr_b)
            i_t = jax.nn.sigmoid(x_conv @ wi_w.T + wi_b)
            a_t = jnp.exp(8.0 * r_t * jax.nn.log_sigmoid(log_a))
            inp = i_t * x_conv
            gate = jnp.sqrt(jnp.maximum(1.0 - a_t * a_t, 0.0))

            def step(h_prev, ts):
                a, g_inp = ts
                h = a * h_prev + g_inp
                return (h, h)
            a_T = jnp.swapaxes(a_t, 0, 1)
            gi_T = jnp.swapaxes(gate * inp, 0, 1)
            h0 = jnp.zeros((B, d), dtype=x.dtype)
            _, hs = jax.lax.scan(step, h0, (a_T, gi_T))
            out = jnp.swapaxes(hs, 0, 1)
            return _rms_norm(out @ ow.T, nw)

        def _reference_tuple_inner(h, down_w, up_w, conv_w, conv_b, Wr_w, Wr_b, Wi_w, Wi_b, log_a, out_w, norm_w):
            B, L, d = h.shape
            M = L // R_STRIDE
            x = h @ down_w.T
            for i in range(N_LAYERS):
                x = _recurrence_layer(x, conv_w[i], conv_b[i], Wr_w[i], Wr_b[i], Wi_w[i], Wi_b[i], log_a[i], out_w[i], norm_w[i])
            encoder_out = x @ up_w.T
            enc_n = _l2_normalize(encoder_out)
            sim = jnp.sum(enc_n[:, 1:] * enc_n[:, :-1], axis=-1)
            p = (1.0 - sim) * 0.5
            boundary_probs = jnp.pad(p, ((0, 0), (1, 0)), constant_values=1.0)
            _, topk_idx = jax.lax.top_k(boundary_probs, M)
            boundary_idx = jnp.sort(topk_idx, axis=1)
            concept_tokens = jnp.take_along_axis(encoder_out, boundary_idx[..., None], axis=1)
            return (concept_tokens, encoder_out, boundary_probs, boundary_probs, boundary_idx)
        return _reference_tuple_inner(h, down_w, up_w, conv_w, conv_b, Wr_w, Wr_b, Wi_w, Wi_b, log_a, out_w, norm_w)[1]

    def _L0_ffn_ref(x, Wr, br, ln_g, ln_b, W1, b1, W2, b2):
        import jax, jax.numpy as jnp
        import numpy as np
        B, S, D, F, E = (4, 512, 256, 1024, 8)
        LN_EPS = 1e-05
        tokens_shape = x.shape[:-1]
        xt = x.reshape(-1, x.shape[-1])
        router_logits = xt @ Wr + br
        router_probs = jax.nn.softmax(router_logits, axis=-1)
        gates = jnp.max(router_probs, axis=-1, keepdims=True)
        idx = jnp.argmax(router_probs, axis=-1)
        onehot = jax.nn.one_hot(idx, E, dtype=xt.dtype)
        mu = jnp.mean(xt, axis=-1, keepdims=True)
        var = jnp.mean(jnp.square(xt - mu), axis=-1, keepdims=True)
        xn = (xt - mu) * jax.lax.rsqrt(var + LN_EPS) * ln_g + ln_b
        h = jnp.einsum('te,td,edf->tf', onehot, xn, W1) + b1[idx]
        h = jax.nn.relu(h)
        y = jnp.einsum('te,tf,efd->td', onehot, h, W2) + b2[idx]
        y = y * gates
        return y.reshape(tokens_shape + (y.shape[-1],))
    x = L0_attn_h
    x = x + 0.5 * _L0_ffn_ref(_layernorm(x, axis=-1), L0_ffn_Wr, L0_ffn_br, L0_ffn_ln_g, L0_ffn_ln_b, L0_ffn_W1, L0_ffn_b1, L0_ffn_W2, L0_ffn_b2)
    x = x + _L0_attn_ref(_layernorm(x, axis=-1), L0_attn_down_w, L0_attn_up_w, L0_attn_conv_w, L0_attn_conv_b, L0_attn_Wr_w, L0_attn_Wr_b, L0_attn_Wi_w, L0_attn_Wi_b, L0_attn_log_a, L0_attn_out_w, L0_attn_norm_w)
    x = x + 0.5 * _L0_ffn_ref(_layernorm(x, axis=-1), L0_ffn_Wr, L0_ffn_br, L0_ffn_ln_g, L0_ffn_ln_b, L0_ffn_W1, L0_ffn_b1, L0_ffn_W2, L0_ffn_b2)
    return x

_drawn_inputs = setup_inputs


def setup_inputs(seed=0):
    import zlib

    import numpy as np

    out = dict(_drawn_inputs(seed))
    spreads = {'L0_attn_conv_b': (0.0, 0.1),
     'L0_attn_Wr_b': (0.0, 2.0),
     'L0_attn_Wi_b': (0.0, 0.8),
     'L0_attn_log_a': (7.5, 0.2),
     'L0_attn_norm_w': (1.0, 0.2),
     'L0_ffn_br': (0.0, 0.288),
     'L0_ffn_ln_g': (1.0, 0.6),
     'L0_ffn_ln_b': (0.0, 2.0),
     'L0_ffn_b1': (0.0, 0.8),
     'L0_ffn_b2': (0.0, 0.407)}
    factors = {'L0_attn_down_w': 64.0, 'L0_attn_Wr_w': 64.0, 'L0_attn_Wi_w': 42.832}
    for name, (base, spread) in spreads.items():
        noise = np.random.default_rng([zlib.crc32(name.encode()), seed]).standard_normal(out[name].shape)
        drawn = base * np.exp(spread * noise) if base else spread * noise
        out[name] = jnp.asarray(drawn.astype(out[name].dtype))
    for name, factor in factors.items():
        out[name] = (out[name] * factor).astype(out[name].dtype)
    return out
```

```python
from contextlib import ExitStack

import concourse.bass as bass
from concourse import mybir

ALU = mybir.AluOpType
ACT = mybir.ActivationFunctionType
F32 = mybir.dt.float32
BF16 = mybir.dt.bfloat16
I32 = mybir.dt.int32
AX = mybir.AxisListType
ds = bass.ds

P = 128
LN_EPS = 1e-5
RMS_EPS = 1e-6
LOG1P_TERMS = 8


def macaron_block(nc, h, down_w, up_w, conv_w, conv_b, gate_r_w, gate_r_b, gate_i_w, gate_i_b, log_a, out_w, norm_w,
                  router_w, router_b, ln_g, ln_b, w1_in, b1_in, w2_in, b2_in, out):
    NB, L, D = h.shape
    NT = NB * L // P
    NC = 4
    TPC = L // NC // P
    CH = L // NC
    KD = D // P
    E = router_w.shape[1]
    F = w1_in.shape[2]
    FC = F // P
    NL, DO = conv_b.shape
    T = NB * L
    REGION = T + P
    SLOTS = (T + E * (P - 1)) // P
    WE = KD * F
    C_MEAN, C_RS, C_GATE, C_ID = D, D + 1, D + 2, D + 3
    RW = D + 4
    RING = 4
    assert NB * DO == P and CH == 512 and FC * D == WE and F == 1024

    x_in = h.rearrange("b l d -> (b l) d")
    x_out = out.rearrange("b l d -> (b l) d")
    routed = nc.dram_tensor("routed_rows", [E * REGION + P, RW], F32, kind="Internal").ap()
    x_mid = nc.dram_tensor("x_after_first_ffn", [T, D], F32, kind="Internal").ap()

    with ExitStack() as ctx:
        def sb(name, shape, dt=F32):
            return ctx.enter_context(nc.sbuf_tensor(name, shape, dt))

        def sem(name):
            return ctx.enter_context(nc.semaphore(name))

        def sems(name, n):
            return [sem(f"{name}{i}") for i in range(n)]

        bank = [ctx.enter_context(nc.psum_tensor(f"bank{i}", [P, 512], F32)) for i in range(8)]

        w1 = sb("w1", [P, E * WE])
        w2 = sb("w2", [P, E * WE])
        rows = sb("rows", [P, NT * RW])
        rows_t = rows[:, :].rearrange("p (t w) -> p t w", w=RW)
        rows_bcj = rows[:, :].rearrange("p (b c j w) -> p b c j w", b=NB, c=NC, j=TPC)
        ident = sb("ident", [P, P])
        wr = sb("wr", [P, KD * E])
        down_t = sb("down_t", [P, KD * DO])
        up_t = sb("up_t", [P, D])
        rec_t = sb("rec_t", [P, 3 * NL * P])
        rec_cur = sb("rec_cur", [P, 3 * P])
        NV = E * FC + 2 * KD + 5 * NL
        vec = sb("vec", [P, NV])
        V_G, V_B = E * FC, E * FC + KD
        V_CB, V_RB, V_IB, V_LA, V_NW = (E * FC + 2 * KD + i * NL for i in range(5))
        U_CB, U_RB, U_IB, U_LS, U_NW, NU = 4, 5, 6, 7, 8, 9
        lay = sb("lay", [P, NL * NU])
        lay_l = lay[:, :].rearrange("p (l u) -> p l u", u=NU)
        cur = sb("cur", [P, NU])
        b2_seq = sb("b2_seq", [P, 3 + L])
        b2_all = b2_seq[:, 0:E * D]
        seq = b2_seq
        rb_all = sb("rb_all", [P, E])
        tri = sb("tri", [P, P], BF16)
        ones = sb("ones", [P, P], BF16)
        half_sel = sb("half_sel", [P, NB])
        e_desc = sb("e_desc", [P, E])
        e_base = sb("e_base", [P, E])
        e_fill = sb("e_fill", [P, E])
        slot_no = sb("slot_no", [P, SLOTS])
        eps_rms = sb("eps_rms", [P, 1])
        quarter = sb("quarter", [P, 1])
        fill = sb("fill", [P, RW])
        minus_half = sb("minus_half", [P, 2 * NB * TPC])
        NJ = NB * TPC
        st = sb("st", [P, NJ * 6])
        mv = sb("mv", [P, NJ * 2])
        var_eps = sb("var_eps", [P, 2 * NJ])
        inv_std = sb("inv_std", [P, 2 * NJ])
        lgt = sb("lgt", [P, NJ * E])
        top = sb("top", [P, NJ])
        hit = sb("hit", [P, NJ * E])
        below = sb("below", [P, NJ * E])
        expo = sb("expo", [P, NJ * E])
        first = sb("first", [P, NJ])
        onehot = sb("onehot", [P, NJ * E], BF16)
        seen = sb("seen", [P, E], BF16)
        group_sum = sb("group_sum", [P, E])
        rank = sb("rank", [P, NJ * E])
        dest_f = sb("dest_f", [P, NJ])
        dest = sb("dest", [P, NT], I32)
        den = sb("den", [P, NJ])
        cnt = sb("cnt", [P, E])
        cnt_i = sb("cnt_i", [P, 2 * E], I32)
        tiles_of = sb("tiles_of", [P, E])
        tile_end = sb("tile_end", [P, E])
        skip = sb("skip", [P, E])
        zero_e = sb("zero_e", [P, E])
        slot_e = sb("slot_e", [P, SLOTS])
        slot_r = sb("slot_r", [P, SLOTS])
        tab_fill = sb("tab_fill", [P, E], I32)
        tab_row = sb("tab_row", [P, SLOTS], I32)
        tab_w = sb("tab_w", [P, SLOTS], I32)
        tab_b = sb("tab_b", [P, SLOTS], I32)
        WORK = 12 * CH
        work = sb("work", [P, WORK])
        vec_rows = work[0:NV, WORK - P:WORK]
        past = work[:, 0:SLOTS * E]
        jump = work[:, SLOTS * E:2 * SLOTS * E]
        xn = work[:, 0:NJ * D].rearrange("p (j d) -> p j d", d=D)
        xn_t = work[:, NJ * D:NJ * D + NB * KD * CH].rearrange("p (b k t) -> p b k t", b=NB, k=KD)

        def at(pos, n):
            return work[:, pos:pos + n]

        pay = [at(i * RW, RW) for i in range(RING)]
        q = RING * RW
        mn = [at(q + i * D, D) for i in range(2)]
        q += 2 * D
        mn_t = [at(q + i * D, D) for i in range(2)]
        q += 2 * D
        hid = at(q, F)
        q += F
        act_t = [at(q + i * F, F) for i in range(2)]
        q += 2 * F
        y_b = at(q, D)
        q += D
        res = [at(q + i * D, D) for i in range(2)]
        q += 2 * D
        assert q <= WORK
        r_xc_b = [at(i * CH, CH) for i in range(2)]
        r_q_b = [at((2 + i) * CH, CH) for i in range(2)]
        r_a_b = [at((4 + i) * CH, CH) for i in range(NC)]
        r_ti_b = [at((8 + i) * CH, CH) for i in range(NC)]
        sq, rms_w = r_xc_b
        up_x = at(8 * CH, CH)
        rms_s = sb("rms_s", [P, TPC * NB])
        rms_i = sb("rms_i", [P, TPC * NB])

        s_par = sem("params_loaded")
        s_x = [sems("x_loaded", NT // TPC), sems("x_mid_loaded", NT // TPC)]
        s_w = sems("expert_loaded", E)
        s_c1 = sem("pool_consts")
        s_c2 = sem("consts_ready")
        s_zero = sem("weights_zeroed")
        s_tp = sem("param_transposed")
        s_tpe = sem("param_kept")
        s_absla = sem("abs_log_a")
        s_expla = sem("exp_log_a")
        s_lsd = sem("log_sigmoid_ready")
        s_mv = sems("moments", 3)
        s_pow = sems("inverse_std", 3)
        s_xn = sems("normalised", 3)
        s_tr = sems("transposed", 3)
        s_te = sems("transposed_kept", 3)
        s_lg = sems("logits", 3)
        s_ex = sems("shifted_logits", 3)
        s_exd = sems("exponentials", 3)
        s_oh = sems("onehot_ready", 3)
        s_rk = sems("rank_ready", 3)
        s_ds = sems("rows_complete", 3)
        s_sc = sems("rows_routed", 3)
        s_seen = sems("seen_final", 3)
        s_cnt = sems("counts_ready", 3)
        s_tab = sems("tables_ready", 3)
        s_fill = sems("regions_filled", 3)
        s_b2 = sem("biases_again")
        s_dn = sem("down_projected")
        s_seq = sem("down_kept")
        s_upx = sem("up_input_staged")
        s_up = sem("up_projected")
        s_add = sem("recurrence_added")
        m_pay = [sems(f"slot_rows{m}_", RING) for m in range(2)]
        m_xn = sems("slot_normalised", 2)
        m_xt = sems("slot_transposed", 2)
        m_xk = sems("slot_affine", 2)
        m_h = sems("hidden_half", 2)
        m_hk = sems("hidden_kept", 2)
        m_ht = sems("hidden_transposed", 2)
        m_a = sems("activated", 2)
        m_y = sems("expert_out", 2)
        m_r = sems("result_ready", 2)
        m_go = sems("stores_begun", 2)
        m_s = [sems(f"result_stored{m}_", RING) for m in range(2)]
        r_w = sem("layer_weights")
        r_c0 = sem("conv_tap3")
        r_xc = sem("conv_done")
        r_g = sem("gates_projected")
        r_ti = sem("gates_activated")
        r_in = sem("input_gated")
        r_aa = sem("decay_squared")
        r_q = sem("gate_square_ready")
        r_gt = sem("input_gate_ready")
        r_h = sem("state_scanned")
        r_y = sem("out_projected")
        r_yk = sem("out_squared")
        r_ss = sem("sum_squares")
        r_sr = sem("rms_root")
        r_si = sem("rms_inverse")
        r_rb = sem("rms_spread")
        r_xx = sem("layer_output")

        N_PAR = 27

        block = ctx.enter_context(nc.Block())

        def tile_of(c, b, j, lo, n):
            return rows[:, ds(c * (TPC * RW) + (b * NC * TPC + j) * RW + lo, n)]

        def column_of(c, col):
            return rows_bcj[:, :, ds(c, 1), :, col:col + 1].rearrange("p b o j w -> p b (o j w)")

        @block.sync
        def _(sp):
            for b in range(NB):
                sp.dma_start(rows_t[:, b * NC * TPC:b * NC * TPC + TPC, 0:D],
                             x_in[b * L:b * L + CH, :].rearrange("(j p) d -> p j d", p=P)).then_inc(s_x[0][b], 16)
            sp.dma_start(wr[:, :].rearrange("p (k e) -> p k e", k=KD),
                         router_w.rearrange("(k p) e -> p k e", p=P)).then_inc(s_par, 16)
            sp.dma_start(rb_all[:, :], router_b[None, :].to_broadcast([P, E])).then_inc(s_par, 16)
            for c in range(1, NC):
                for b in range(NB):
                    t0 = (b * NC + c) * TPC
                    sp.dma_start(rows_t[:, t0:t0 + TPC, 0:D],
                                 x_in[t0 * P:(t0 + TPC) * P, :].rearrange("(j p) d -> p j d", p=P)
                                 ).then_inc(s_x[0][c * NB + b], 16)
            for e in range(E):
                sp.dma_start(w1[:, e * WE:(e + 1) * WE].rearrange("p (k f) -> p k f", k=KD),
                             w1_in[e].rearrange("(k p) f -> p k f", p=P)).then_inc(s_w[e], 16)
                sp.dma_start(w2[:, e * WE:(e + 1) * WE].rearrange("p (c d) -> p c d", c=FC),
                             w2_in[e].rearrange("(c p) d -> p c d", p=P)).then_inc(s_w[e], 16)
            sp.wait_ge(s_c2, 1)
            sp.dma_start(routed[E * REGION:E * REGION + P, :], fill[:, :]).then_inc(s_fill[0], 16)

            def feed_slots(m, phase):
                sp.wait_ge(s_tab[phase], 1)
                for e in range(E):
                    row = sp.value_load(tab_fill[0:1, e:e + 1], min_val=0, max_val=E * REGION - P)
                    sp.dma_start(routed[ds(row, P), :], fill[:, :]).then_inc(s_fill[phase], 16)
                sp.wait_ge(s_fill[phase], 16 * (E + (phase == 0)))
                sp.wait_ge(s_sc[phase], 16 * NT)

                def slot(t, i, s, reuse):
                    row = sp.value_load(tab_row[0:1, ds(t, 1)], min_val=0, max_val=E * REGION)
                    if reuse:
                        sp.wait_ge(m_s[m][s], i * 16)
                    sp.dma_start(pay[s], routed[ds(row, P), :]).then_inc(m_pay[m][s], 16)

                for s in range(RING):
                    slot(s, 0, s, False)
                with sp.Fori(1, SLOTS // RING) as i:
                    for s in range(RING):
                        slot(i * RING + s, i, s, True)
                for s in range(SLOTS % RING):
                    slot(SLOTS // RING * RING + s, SLOTS // RING, s, True)

            feed_slots(0, 0)
            for s in range(RING):
                sp.wait_ge(m_s[0][s], 16 * ((SLOTS - s + RING - 1) // RING))
            for c in range(NC):
                for b in range(NB):
                    t0 = (b * NC + c) * TPC
                    sp.dma_start(rows_t[:, t0:t0 + TPC, 0:D],
                                 x_mid[t0 * P:(t0 + TPC) * P, :].rearrange("(j p) d -> p j d", p=P)
                                 ).then_inc(s_x[1][c * NB + b], 16)
            sp.wait_ge(s_upx, NC)
            sp.dma_start(b2_all, b2_in.rearrange("e d -> (e d)")[None, :].to_broadcast([P, E * D])).then_inc(s_b2, 16)
            feed_slots(1, 2)
            for s in range(RING):
                sp.wait_ge(m_s[1][s], 16 * ((SLOTS - s + RING - 1) // RING))

        @block.gpsimd
        def _(pool):
            g = nc.gpsimd
            g.memset(ident[:, :], 0.0)
            g.memset(rec_t[:, 0:P], 1.0)
            g.memset(rec_t[:, P:2 * P], 1.0)
            g.iota(tab_w[:, 0:SLOTS], [[1, SLOTS]], base=0, channel_multiplier=0)
            g.iota(cnt_i[:, 0:E], [[-1, E]], base=E, channel_multiplier=0)
            g.iota(tab_fill[:, :], [[REGION, E]], base=0, channel_multiplier=0)
            g.iota(cnt_i[:, E:2 * E], [[REGION, E]], base=0, channel_multiplier=1)
            g.iota(rows_t[:, :, C_ID:C_ID + 1].bitcast(I32).rearrange("p t w -> p (t w)"), [[P, NT]], base=0,
                   channel_multiplier=1)
            g.memset(fill[:, 0:C_ID], 0.0)
            g.iota(fill[:, C_ID:C_ID + 1].bitcast(I32), [[0, 1]], base=T, channel_multiplier=1)
            g.memset(minus_half[:, :], -0.5)
            g.memset(eps_rms[:, :], RMS_EPS)
            g.memset(quarter[:, :], 0.25)
            g.memset(zero_e[:, :], 0.0)
            g.memset(half_sel[:, :], 0.0)
            pool.drain()
            for b in range(NB):
                g.memset(half_sel[b * DO:(b + 1) * DO, b:b + 1], 1.0)
                pool.drain()
            g.affine_select(out=ident[:, :], in_=ident[:, :], compare_op=ALU.not_equal, fill=1.0, base=0,
                            pattern=[[-1, P]], channel_multiplier=1)
            g.affine_select(out=rec_t[:, 0:P], in_=rec_t[:, 0:P], compare_op=ALU.is_ge, fill=0.0, base=-1,
                            pattern=[[1, P]], channel_multiplier=-1).then_inc(s_c1, 1)

            def powers(phase, c):
                pool.wait_ge(s_mv[phase], c + 1)
                v = mv[:, :].rearrange("p (j s) -> p j s", s=2)[:, :, 1]
                g.tensor_scalar(var_eps[:, 0:NJ], v, 1.0, LN_EPS, ALU.mult, ALU.add)
                g.tensor_scalar(var_eps[:, NJ:2 * NJ], v, 1.0 + LN_EPS, LN_EPS * LN_EPS, ALU.mult, ALU.add)
                pool.drain()
                g.tensor_tensor(inv_std[:, :], var_eps[:, :], minus_half[:, :], ALU.pow).then_inc(s_pow[phase], 1)

            def route(phase, c):
                pool.wait_ge(s_ds[phase], c + 1)
                for b in range(NB):
                    for j in range(TPC):
                        t = (b * NC + c) * TPC + j
                        g.indirect_dma_start(
                            out=routed, out_offset=bass.IndirectOffsetOnAxis(ap=dest[:, t:t + 1], axis=0),
                            in_=rows[:, t * RW:(t + 1) * RW], in_offset=None,
                            bounds_check=E * REGION - 1, oob_is_err=False).then_inc(s_sc[phase], 16)

            def store_slots(m):
                target = x_mid if m == 0 else x_out
                last_token = pool.to_reg(T - 1)

                def slot(t, s):
                    pool.wait_ge(m_r[m], t + 1)
                    pool.sem_inc(m_go[m])
                    g.indirect_dma_start(
                        out=target, out_offset=bass.IndirectOffsetOnAxis(ap=pay[s][:, C_ID:C_ID + 1].bitcast(I32),
                                                                         axis=0),
                        in_=res[s % 2], in_offset=None, bounds_check=last_token, oob_is_err=False
                    ).then_inc(m_s[m][s], 16)

                with pool.Fori(0, SLOTS // RING) as i:
                    for s in range(RING):
                        slot(i * RING + s, s)
                for s in range(SLOTS % RING):
                    slot(SLOTS // RING * RING + s, s)

            for c in range(NC):
                powers(0, c)
                if c:
                    route(0, c - 1)
            route(0, NC - 1)
            store_slots(0)
            for c in range(NC):
                powers(1, c)
            with pool.Fori(0, NL) as l:
                for c in range(NC):
                    pool.wait_ge(r_ti, l * NC + c + 1)
                    pool.wait_ge(r_h, l * NC + max(c, 1))
                    g.tensor_tensor(r_q_b[c % 2], r_a_b[c], r_a_b[c], ALU.mult).then_inc(r_aa, 1)
            for c in range(NC):
                pool.wait_ge(r_xx, NL * NC + 1)
                if c:
                    pool.wait_ge(s_up, 2 * NB * c)
                g.tensor_copy(up_x, seq[:, 3 + c * CH:3 + (c + 1) * CH]).then_inc(s_upx, 1)
                powers(2, c)
                if c:
                    route(2, c - 1)
            route(2, NC - 1)
            store_slots(1)

        @block.vector
        def _(dve):
            v = nc.vector

            v.memset(work[:, 0:3 * NL * P], 0.0).then_inc(s_zero, 1)
            dve.wait_ge(s_c1, 1)
            v.tensor_copy(tri[:, :], rec_t[:, 0:P])
            v.tensor_copy(ones[:, :], rec_t[:, P:2 * P])
            v.tensor_copy(slot_no[:, :], tab_w[:, :])
            v.tensor_copy(e_desc[:, :], cnt_i[:, 0:E])
            v.tensor_copy(e_base[:, :], tab_fill[:, :])
            v.tensor_copy(e_fill[:, :], cnt_i[:, E:2 * E]).then_inc(s_c2, 1)

            def moments(phase, c, waits):
                for b in range(NB):
                    for j in range(TPC):
                        if waits and j == 0:
                            waits(c, b)
                        jj = b * TPC + j
                        v.bn_stats(st[:, jj * 6:jj * 6 + 6], tile_of(c, b, j, 0, D))
                dve.drain()
                if not (isinstance(c, int) and c == 0):
                    pass
                for jj in range(NJ):
                    last = v.bn_aggr(mv[:, jj * 2:jj * 2 + 2], st[:, jj * 6:jj * 6 + 6])
                last.then_inc(s_mv[phase], 1)

            def normalise(phase, c, guard):
                dve.wait_ge(s_pow[phase], c + 1)
                if guard:
                    dve.wait_ge(s_tr[phase], c * 4)
                for b in range(NB):
                    for j in range(TPC):
                        jj = b * TPC + j
                        v.tensor_scalar(xn[:, jj, :], tile_of(c, b, j, 0, D), mv[:, 2 * jj:2 * jj + 1],
                                        inv_std[:, jj:jj + 1], ALU.subtract, ALU.mult)
                mean = mv[:, :].rearrange("p (b j s) -> p b j s", b=NB, s=2)[:, :, :, 0]
                v.tensor_copy(column_of(c, C_MEAN), mean)
                v.tensor_copy(column_of(c, C_RS),
                              inv_std[:, NJ:2 * NJ].rearrange("p (b j) -> p b j", b=NB)).then_inc(s_xn[phase], 1)

            def jx(a):
                return a[:, :].rearrange("p (j e) -> p j e", e=E)

            def per_e(a):
                return a[:, None, :].to_broadcast([P, NJ, E])

            def per_j(a):
                return a[:, :, None].to_broadcast([P, NJ, E])

            def choose(phase, c):
                dve.wait_ge(s_lg[phase], c + 1)
                v.tensor_tensor(jx(lgt), bank[4][:, 0:NJ * E].rearrange("p (j e) -> p j e", e=E), per_e(rb_all), ALU.add)
                dve.drain()
                v.tensor_reduce(top[:, :], jx(lgt), AX.X, ALU.max)
                dve.drain()
                v.tensor_tensor(jx(below), jx(lgt), per_j(top), ALU.subtract).then_inc(s_ex[phase], 1)
                v.tensor_tensor(jx(hit), jx(lgt), per_j(top), ALU.is_equal)
                dve.drain()
                v.tensor_tensor(jx(hit), jx(hit), per_e(e_desc), ALU.mult)
                dve.drain()
                v.tensor_reduce(first[:, :], jx(hit), AX.X, ALU.max)
                dve.drain()
                v.tensor_tensor(jx(onehot), per_j(first), per_e(e_desc), ALU.is_equal).then_inc(s_oh[phase], 1)
                dve.wait_ge(s_exd[phase], c + 1)
                v.tensor_reduce(den[:, :], jx(expo), AX.X, ALU.add)
                dve.drain()
                v.tensor_reduce(group_sum[:, :], onehot[:, :].rearrange("p (j e) -> p e j", e=E), AX.X, ALU.add)
                v.reciprocal(top[:, :], den[:, :])
                dve.drain()
                v.tensor_scalar(column_of(c, C_GATE), top[:, :].rearrange("p (b j) -> p b j", b=NB), 0.5, None, ALU.mult)
                dve.wait_ge(s_rk[phase], c + 1)
                v.tensor_tensor(seen[:, :], seen[:, :], group_sum[:, :], ALU.add)
                v.tensor_tensor(jx(rank), bank[5][:, 0:NJ * E].rearrange("p (j e) -> p j e", e=E), per_e(e_base), ALU.add)
                dve.drain()
                v.tensor_tensor(jx(rank), jx(rank), jx(onehot), ALU.mult)
                dve.drain()
                v.tensor_reduce(dest_f[:, :], jx(rank), AX.X, ALU.add)
                dve.drain()
                d = dest[:, :].rearrange("p (b c j) -> p b c j", b=NB, c=NC)[:, :, ds(c, 1), :].rearrange(
                    "p b o j -> p b (o j)")
                v.tensor_copy(d, dest_f[:, :].rearrange("p (b j) -> p b j", b=NB)).then_inc(s_ds[phase], 1)

            def tables(phase):
                dve.wait_ge(s_cnt[phase], 1)
                v.tensor_copy(cnt[:, :], bank[6][:, 0:E])
                v.tensor_scalar(cnt_i[:, 0:E], bank[6][:, 0:E], float(P - 1), None, ALU.add)
                dve.drain()
                v.tensor_tensor(tab_fill[:, :], cnt[:, :], e_base[:, :], ALU.add)
                v.tensor_scalar(cnt_i[:, E:2 * E], cnt_i[:, 0:E], P.bit_length() - 1, None, ALU.logical_shift_right)
                dve.drain()
                v.tensor_copy(tiles_of[:, :], cnt_i[:, E:2 * E])
                dve.drain()
                v.tensor_tensor_scan(tile_end[:, :], tiles_of[:, :], zero_e[:, :], 0.0, ALU.add, ALU.add)
                v.tensor_scalar(skip[:, :], tiles_of[:, :], -float(P), float(REGION), ALU.mult, ALU.add)
                dve.drain()
                ps = past.rearrange("p (t e) -> p t e", e=E)
                jp = jump.rearrange("p (t e) -> p t e", e=E)
                v.tensor_tensor(ps, slot_no[:, :, None].to_broadcast([P, SLOTS, E]),
                                tile_end[:, None, :].to_broadcast([P, SLOTS, E]), ALU.is_ge)
                dve.drain()
                v.tensor_reduce(slot_e[:, :], ps, AX.X, ALU.add)
                v.tensor_tensor(jp, ps, skip[:, None, :].to_broadcast([P, SLOTS, E]), ALU.mult)
                dve.drain()
                v.tensor_reduce(slot_r[:, :], jp, AX.X, ALU.add)
                v.tensor_scalar(slot_e[:, :], slot_e[:, :], float(E - 1), float(WE), ALU.min, ALU.mult)
                dve.drain()
                v.scalar_tensor_tensor(out=slot_r[:, :], in0=slot_no[:, :], scalar=float(P), in1=slot_r[:, :],
                                       op0=ALU.mult, op1=ALU.add)
                v.tensor_copy(tab_w[:, :], slot_e[:, :])
                v.tensor_scalar(tab_b[:, :], slot_e[:, :], float(FC) / WE, None, ALU.mult)
                dve.drain()
                v.tensor_scalar(tab_row[:, :], slot_r[:, :], float(E * REGION), None, ALU.min).then_inc(s_tab[phase], 1)
                dve.drain()

            def routing(phase, before):
                v.memset(seen[:, :], 0.0)
                before(0)
                moments(phase, 0, None)
                normalise(phase, 0, False)

                def step(c, guard):
                    before(c + 1)
                    moments(phase, c + 1, None)
                    choose(phase, c)
                    normalise(phase, c + 1, guard)

                for c in range(NC - 1):
                    step(c, True)
                choose(phase, NC - 1)
                dve.drain()
                v.tensor_copy(top[:, 0:1], dest_f[:, 0:1]).then_inc(s_seen[phase], 1)
                tables(phase)

            def slots(m):
                def norm(t, i, s):
                    dve.wait_ge(m_pay[m][s], i * 16 + 16)
                    p = pay[s]
                    v.tensor_scalar(mn[s % 2], p[:, 0:D], p[:, C_MEAN:C_MEAN + 1], p[:, C_RS:C_RS + 1],
                                    ALU.subtract, ALU.mult).then_inc(m_xn[m], 1)

                def activate(t, s):
                    eb = dve.value_load(tab_b[0:1, ds(t, 1)], min_val=0, max_val=(E - 1) * FC)
                    for c in range(FC):
                        if c % 4 == 0:
                            dve.wait_ge(m_ht[m], t * 2 + c // 4 + 1)
                        last = v.tensor_scalar(act_t[s % 2][:, c * P:(c + 1) * P],
                                               bank[3 + c // 4][:, c % 4 * P:(c % 4 + 1) * P],
                                               vec[:, ds(eb + c, 1)], 0.0, ALU.add, ALU.max)
                    last.then_inc(m_a[m], 1)

                def finish(t, s, stored):
                    eb = dve.value_load(tab_b[0:1, ds(t, 1)], min_val=0, max_val=(E - 1) * FC)
                    dve.wait_ge(m_y[m], t + 1)
                    v.tensor_tensor(y_b, bank[5][:, 0:D], b2_all[:, ds(eb * (D // FC), D)], ALU.add)
                    dve.drain()
                    if stored is not None:
                        dve.wait_ge(m_s[m][(s + 2) % RING], stored)
                    v.scalar_tensor_tensor(out=res[s % 2], in0=y_b, scalar=pay[s][:, C_GATE:C_GATE + 1],
                                           in1=pay[s][:, 0:D], op0=ALU.mult, op1=ALU.add).then_inc(m_r[m], 1)

                def step(t, i, s, more=True, stored=True):
                    if more:
                        norm(t + 1, i + (s + 1) // RING, (s + 1) % RING)
                    sp_, ip = (s - 1) % RING, i - (s == 0)
                    k = (ip * 16 + 16 if sp_ >= 2 else ip * 16) - (16 if False else 0)
                    if sp_ >= 2:
                        k = ip * 16 + 16
                    else:
                        k = ip * 16
                    finish(t - 1, sp_, k if stored else None)
                    activate(t, s)

                if m == 1:
                    dve.wait_ge(s_b2, 16)
                norm(0, 0, 0)
                norm(1, 0, 1)
                activate(0, 0)
                step(1, 0, 1, stored=False)
                step(2, 0, 2, stored=False)
                step(3, 0, 3)
                with dve.Fori(1, SLOTS // RING) as i:
                    for s in range(RING):
                        step(i * RING + s, i, s)
                n = SLOTS // RING
                for s in range(SLOTS % RING):
                    step(n * RING + s, n, s, more=s < SLOTS % RING - 1)
                t = SLOTS - 1
                finish(t, t % RING, (t - 2) // RING * 16 + 16)

            def x_arrives(c):
                for b in range(NB):
                    dve.wait_ge(s_x[0][c * NB + b], 16)

            dve.wait_ge(s_tpe, 1)
            la = vec[:, V_LA:V_LA + NL]
            a0, a1, a2, a3 = (hit[:, 8 * i:8 * i + NL] for i in range(4))
            v.tensor_copy(lay_l[:, :, U_CB], vec[:, V_CB:V_CB + NL])
            v.tensor_copy(lay_l[:, :, U_NW], vec[:, V_NW:V_NW + NL])
            v.tensor_scalar(lay_l[:, :, U_RB], vec[:, V_RB:V_RB + NL], 0.5, None, ALU.mult)
            v.tensor_scalar(lay_l[:, :, U_IB], vec[:, V_IB:V_IB + NL], 0.5, None, ALU.mult)
            v.scalar_tensor_tensor(out=a0, in0=la, scalar=-1.0, in1=la, op0=ALU.mult, op1=ALU.max).then_inc(s_absla, 1)
            dve.wait_ge(s_expla, 1)
            v.tensor_scalar(a2, a1, 2.0, None, ALU.add)
            dve.drain()
            v.reciprocal(a3, a2)
            dve.drain()
            v.tensor_tensor(a1, a1, a3, ALU.mult)
            dve.drain()
            v.tensor_tensor(a2, a1, a1, ALU.mult)
            dve.drain()
            v.tensor_scalar(a3, a2, 1.0 / (2 * LOG1P_TERMS + 1), None, ALU.mult)
            for k in range(LOG1P_TERMS - 1, 0, -1):
                dve.drain()
                v.scalar_tensor_tensor(out=a3, in0=a3, scalar=1.0 / (2 * k + 1), in1=a2, op0=ALU.add, op1=ALU.mult)
            dve.drain()
            v.scalar_tensor_tensor(out=a3, in0=a3, scalar=1.0, in1=a1, op0=ALU.add, op1=ALU.mult)
            v.tensor_scalar(a0, la, 0.0, 4.0, ALU.min, ALU.mult)
            dve.drain()
            v.scalar_tensor_tensor(out=lay_l[:, :, U_LS], in0=a3, scalar=-8.0, in1=a0, op0=ALU.mult, op1=ALU.add
                                   ).then_inc(s_lsd, 1)

            dve.wait_ge(s_par, 16 * N_PAR)
            routing(0, x_arrives)
            slots(0)

            def mid_arrives(c):
                for b in range(NB):
                    dve.wait_ge(s_x[1][c * NB + b], 16)

            mid_arrives(0)
            moments(1, 0, None)
            normalise(1, 0, False)
            for c in range(1, NC):
                mid_arrives(c)
                moments(1, c, None)
                normalise(1, c, True)

            dve.wait_ge(s_seq, NC)
            v.memset(seq[:, 0:3], 0.0).then_inc(r_xx, 1)
            v.memset(rms_i[:, :], 0.0).then_inc(r_h, 1)
            dve.drain()

            def convolve(l, c):
                xc = r_xc_b[c % 2]
                dve.wait_ge(r_c0, l * NC + c + 1)
                for k in range(2, -1, -1):
                    last = v.scalar_tensor_tensor(out=xc, in0=seq[:, c * CH + k:c * CH + k + CH],
                                                  scalar=cur[:, k:k + 1], in1=xc, op0=ALU.mult, op1=ALU.add)
                    if k:
                        dve.drain()
                last.then_inc(r_xc, 1)

            def gate_input(l, c):
                dve.wait_ge(r_ti, l * NC + c + 1)
                v.scalar_tensor_tensor(out=r_ti_b[c], in0=r_ti_b[c], scalar=1.0, in1=r_xc_b[c % 2],
                                       op0=ALU.add, op1=ALU.mult).then_inc(r_in, 1)

            def clamp(l, c):
                dve.wait_ge(r_aa, l * NC + c + 1)
                v.tensor_scalar(r_q_b[c % 2], r_q_b[c % 2], 1.0, None, ALU.min).then_inc(r_q, 1)

            def scan(l, c):
                dve.wait_ge(r_gt, l * NC + c + 1)
                v.tensor_tensor(r_q_b[c % 2], r_q_b[c % 2], r_ti_b[c], ALU.mult)
                dve.drain()
                prev = 0.0 if c == 0 else r_a_b[c - 1][:, CH - 1:CH]
                v.tensor_tensor_scan(r_a_b[c], r_a_b[c], r_q_b[c % 2], prev, ALU.mult, ALU.add).then_inc(r_h, 1)

            def inverse(l, c):
                dve.wait_ge(r_sr, l * NC + c + 1)
                v.reciprocal(rms_i[:, :], rms_s[:, :])
                dve.drain()
                w = rms_w.rearrange("p (g n) -> p g n", n=DO)
                v.tensor_copy(w, rms_i[:, :, None].to_broadcast([P, TPC * NB, DO])).then_inc(r_si, 1)

            def rescale(l, c):
                dve.wait_ge(r_rb, l * NC + c + 1)
                v.tensor_tensor(seq[:, 3 + c * CH:3 + (c + 1) * CH], r_ti_b[c], bank[6][:, :], ALU.mult
                                ).then_inc(r_xx, 1)

            with dve.Fori(0, NL) as l:
                for c in range(NC):
                    convolve(l, c)
                    if c:
                        gate_input(l, c - 1)
                gate_input(l, NC - 1)
                clamp(l, 0)
                for c in range(NC):
                    if c + 1 < NC:
                        clamp(l, c + 1)
                    scan(l, c)
                    if c:
                        inverse(l, c - 1)
                        rescale(l, c - 1)
                inverse(l, NC - 1)
                rescale(l, NC - 1)
                dve.drain()

            def recurrence_arrives(c):
                for b in range(NB):
                    for hh in range(2):
                        n = (c * NB + b) * 2 + hh
                        dve.wait_ge(s_up, n + 1)
                        r = rows_t[:, (b * NC + c) * TPC + 2 * hh:(b * NC + c) * TPC + 2 * hh + 2, 0:D]
                        v.tensor_tensor(r, r, bank[7 if hh else 6][:, :].rearrange("p (j d) -> p j d", d=D), ALU.add
                                        ).then_inc(s_add, 1)
                dve.drain()

            routing(2, recurrence_arrives)
            slots(1)

        @block.scalar
        def _(act):
            a = nc.scalar
            n_par = [2]

            def load(dst, src):
                act.dma_start(dst, src).then_inc(s_par, 16)
                n_par[0] += 1

            load(vec_rows[0:E * FC, :], b1_in.rearrange("e (c p) -> (e c) p", p=P))
            load(vec_rows[V_G:V_G + KD, :], ln_g.rearrange("(k p) -> k p", p=P))
            load(vec_rows[V_B:V_B + KD, :], ln_b.rearrange("(k p) -> k p", p=P))
            for pos, src in ((V_CB, conv_b), (V_RB, gate_r_b), (V_IB, gate_i_b), (V_LA, log_a), (V_NW, norm_w)):
                for b in range(NB):
                    load(vec_rows[pos:pos + NL, b * DO:(b + 1) * DO], src)
            for b in range(NB):
                load(lay_l[b * DO:(b + 1) * DO, :, 0:4], conv_w.rearrange("l c k -> c l k"))
            load(b2_all, b2_in.rearrange("e d -> (e d)")[None, :].to_broadcast([P, E * D]))
            act.wait_ge(s_zero, 1)
            nat = work[:, 0:3 * NL * P].rearrange("p (m l i) -> p m l i", m=3, l=NL)
            for m, src in enumerate((gate_r_w, gate_i_w, out_w)):
                for b in range(NB):
                    load(nat[b * DO:(b + 1) * DO, m, :, b * DO:(b + 1) * DO], src.rearrange("l o i -> o l i"))
            load(work[0:DO, 3 * NL * P:3 * NL * P + D], down_w)
            upn = work[:, 3 * NL * P + D:3 * NL * P + 2 * D].rearrange("p (k b i) -> p k b i", k=KD, b=NB)
            for b in range(NB):
                load(upn[:, :, b, :], up_w.rearrange("(k p) i -> p k i", p=P))
            assert n_par[0] == N_PAR, n_par[0]

            act.wait_ge(s_tp, 1)
            a.activation(vec[:, :], bank[0][:, 0:NV], ACT.Copy).then_inc(s_tpe, 1)
            for m in range(3):
                a.activation(rec_t[:, m * NL * P:(m + 1) * NL * P], bank[1 + m][:, 0:NL * P], ACT.Copy)
            a.activation(down_t[:, :], bank[4][:, 0:KD * DO], ACT.Copy)
            a.activation(up_t[:, :], bank[5][:, 0:D], ACT.Copy).then_inc(s_tpe, 1)
            act.wait_ge(s_absla, 1)
            a.activation(hit[:, 8:8 + NL], hit[:, 0:NL], ACT.Exp, scale=-1.0).then_inc(s_expla, 1)

            def keep(phase, c, guard):
                for n in range(NB * KD):
                    act.wait_ge(s_tr[phase], c * 4 + n + 1)
                    if n == 0 and guard:
                        act.wait_ge(s_lg[phase] if phase != 1 else s_dn, c)
                    a.activation(xn_t[:, n // KD, n % KD, :], bank[n][:, :], ACT.Copy).then_inc(s_te[phase], 1)

            def exponentials(phase, c):
                act.wait_ge(s_ex[phase], c + 1)
                a.activation(expo[:, :], below[:, :], ACT.Exp).then_inc(s_exd[phase], 1)

            def routing(phase):
                keep(phase, 0, False)
                exponentials(phase, 0)
                with act.Fori(1, NC) as c:
                    keep(phase, c, True)
                    exponentials(phase, c)

            def slots(m):
                def affine(t, s, guard=True):
                    act.wait_ge(m_xt[m], t + 1)
                    for k in range(KD):
                        last = a.activation(mn_t[s % 2][:, k * P:(k + 1) * P], bank[0][:, k * P:(k + 1) * P], ACT.Identity,
                                            scale=vec[:, V_G + k:V_G + k + 1], bias=vec[:, V_B + k:V_B + k + 1])
                    last.then_inc(m_xk[m], 1)

                def hidden(t):
                    for n in range(2):
                        act.wait_ge(m_h[m], t * 2 + n + 1)
                        a.activation(hid[:, n * 512:(n + 1) * 512], bank[1 + n][:, :], ACT.Copy).then_inc(m_hk[m], 1)

                affine(0, 0)
                hidden(0)
                affine(1, 1)
                with act.Fori(0, (SLOTS - 3) // 2) as i:
                    for s in range(2):
                        hidden(i * 2 + 1 + s)
                        affine(i * 2 + 2 + s, s)
                hidden(SLOTS - 2)
                affine(SLOTS - 1, (SLOTS - 1) % 2)
                hidden(SLOTS - 1)

            routing(0)
            slots(0)
            for c in range(NC):
                keep(1, c, c > 0)
                act.wait_ge(s_dn, c + 1)
                a.activation(seq[:, 3 + c * CH:3 + (c + 1) * CH], bank[4][:, :], ACT.Copy).then_inc(s_seq, 1)
            act.wait_ge(s_lsd, 1)
            act.drain()

            with act.Fori(0, NL) as l:
                for m in range(3):
                    a.activation(rec_cur[:, m * P:(m + 1) * P], rec_t[:, ds(l * P + m * NL * P, P)], ACT.Copy
                                 ).then_inc(r_w, 1)
                a.activation(cur[:, :], lay[:, ds(l * NU, NU)], ACT.Copy)
                act.drain()

                def tap(c):
                    if c == 0:
                        act.wait_ge(r_xx, l * NC + 1)
                    elif c >= 2:
                        act.wait_ge(r_in, l * NC + c - 1)
                    a.activation(r_xc_b[c % 2], seq[:, 3 + c * CH:3 + (c + 1) * CH], ACT.Identity,
                                 scale=cur[:, 3:4], bias=cur[:, U_CB:U_CB + 1]).then_inc(r_c0, 1)

                def gates(c):
                    act.wait_ge(r_g, (l * NC + c) * 2 + 2)
                    a.activation(r_a_b[c], bank[c % 2][:, :], ACT.Tanh, scale=0.5, bias=cur[:, U_RB:U_RB + 1])
                    a.activation(r_ti_b[c], bank[2 + c % 2][:, :], ACT.Tanh, scale=0.5,
                                 bias=cur[:, U_IB:U_IB + 1])
                    act.drain()
                    a.activation(r_a_b[c], r_a_b[c], ACT.Exp, scale=cur[:, U_LS:U_LS + 1],
                                 bias=cur[:, U_LS:U_LS + 1]).then_inc(r_ti, 1)

                def root(c):
                    act.wait_ge(r_q, l * NC + c + 1)
                    a.activation(r_q_b[c % 2], r_q_b[c % 2], ACT.Sqrt, scale=-0.25, bias=quarter[:, :]
                                 ).then_inc(r_gt, 1)

                def squares(c):
                    act.wait_ge(r_y, l * NC + c + 1)
                    if c:
                        act.wait_ge(r_ss, l * NC + c)
                    a.activation(r_ti_b[c], bank[4 + c % 2][:, :], ACT.Copy, scale=cur[:, U_NW:U_NW + 1])
                    a.activation(sq, bank[4 + c % 2][:, :], ACT.Square).then_inc(r_yk, 1)

                def rms(c):
                    act.wait_ge(r_ss, l * NC + c + 1)
                    a.activation(rms_s[:, :], bank[7][:, 0:TPC * NB], ACT.Sqrt, scale=1.0 / DO, bias=eps_rms[:, :]
                                 ).then_inc(r_sr, 1)

                tap(0)
                tap(1)
                for c in range(NC):
                    gates(c)
                    if c + 2 < NC:
                        tap(c + 2)
                root(0)
                for c in range(NC):
                    if c + 1 < NC:
                        root(c + 1)
                    squares(c)
                    rms(c)
                act.wait_ge(r_xx, l * NC + NC + 1)
            routing(2)
            slots(1)

        @block.tensor
        def _(pe):
            t = nc.tensor
            pe.wait_ge(s_par, 16 * N_PAR)
            pe.wait_ge(s_c2, 1)
            t.transpose(bank[0][:, 0:NV], vec_rows, ident[0:NV, 0:NV])
            for m in range(3):
                for l in range(NL):
                    t.transpose(bank[1 + m][:, l * P:(l + 1) * P], work[:, (m * NL + l) * P:(m * NL + l + 1) * P],
                                ident[:, :])
            q = 3 * NL * P
            for k in range(KD):
                t.transpose(bank[4][:, k * DO:(k + 1) * DO], work[0:DO, q + k * P:q + (k + 1) * P], ident[0:DO, 0:DO])
            for k in range(KD):
                last = t.transpose(bank[5][:, k * P:(k + 1) * P], work[:, q + D + k * P:q + D + (k + 1) * P],
                                   ident[:, :])
            last.then_inc(s_tp, 1)

            def transposes(phase, c, first):
                pe.wait_ge(s_xn[phase], c + 1)
                for b in range(NB):
                    for k in range(KD):
                        n = b * KD + k
                        if not first:
                            pe.wait_ge(s_te[phase], (c - 1) * 4 + n + 1)
                        for j in range(TPC):
                            last = t.transpose(bank[n][:, j * P:(j + 1) * P],
                                               xn[:, b * TPC + j, k * P:(k + 1) * P], ident[:, :])
                        last.then_inc(s_tr[phase], 1)

            def logits(phase, c):
                pe.wait_ge(s_te[phase], c * 4 + 4)
                for b in range(NB):
                    for j in range(TPC):
                        o = (b * TPC + j) * E
                        for k in range(KD):
                            last = t.matmul(bank[4][:, o:o + E], xn_t[:, b, k, j * P:(j + 1) * P],
                                            wr[:, k * E:(k + 1) * E], start=k == 0, stop=k == KD - 1)
                last.then_inc(s_lg[phase], 1)

            def ranks(phase, c):
                pe.wait_ge(s_oh[phase], c + 1)
                o3 = bank[5][:, 0:NJ * E]
                t.matmul(o3, tri[:, :], onehot[:, :], start=True, stop=False)
                t.matmul(o3.rearrange("p (j e) -> p j e", e=E), ones[:, :],
                         seen[:, None, :].to_broadcast([P, NJ, E]), start=False, stop=False)
                for j in range(NJ - 1):
                    last = t.matmul(bank[5][:, (j + 1) * E:NJ * E].rearrange("p (j e) -> p j e", e=E), ones[:, :],
                                    onehot[:, None, j * E:(j + 1) * E].to_broadcast([P, NJ - 1 - j, E]),
                                    start=False, stop=j == NJ - 2)
                last.then_inc(s_rk[phase], 1)

            def up(c):
                pe.wait_ge(s_upx, c + 1)
                for b in range(NB):
                    for hh in range(2):
                        n = (c * NB + b) * 2 + hh
                        if n >= 2:
                            pe.wait_ge(s_add, n - 1)
                        for j in range(2):
                            jj = 2 * hh + j
                            last = t.matmul(bank[7 if hh else 6][:, j * D:(j + 1) * D],
                                            up_x[b * DO:(b + 1) * DO, jj * P:(jj + 1) * P],
                                            up_t[b * DO:(b + 1) * DO, :], start=True, stop=True)
                        last.then_inc(s_up, 1)

            def routing(phase):
                if phase == 2:
                    up(0)
                transposes(phase, 0, True)
                for c in range(NC):
                    logits(phase, c)
                    if phase == 2 and c + 1 < NC:
                        up(c + 1)
                    ranks(phase, c)
                    if c + 1 < NC:
                        transposes(phase, c + 1, False)
                pe.wait_ge(s_seen[phase], 1)
                t.matmul(bank[6][:, 0:E], ones[:, :], seen[:, :], start=True, stop=True).then_inc(s_cnt[phase], 1)

            def slots(m):
                def turn_input(i, s, first=False):
                    pe.wait_ge(m_xn[m], i + 1)
                    if not first:
                        pe.wait_ge(m_xk[m], i)
                    for k in range(KD):
                        last = t.transpose(bank[0][:, k * P:(k + 1) * P], mn[s][:, k * P:(k + 1) * P], ident[:, :])
                    last.then_inc(m_xt[m], 1)

                def weights_of(i):
                    return pe.value_load(tab_w[0:1, ds(i, 1)], min_val=0, max_val=(E - 1) * WE)

                def hidden(i, s, w, first=False):
                    pe.wait_ge(m_xk[m], i + 1)
                    for n in range(2):
                        if not first:
                            pe.wait_ge(m_hk[m], (i - 1) * 2 + n + 1)
                        for k in range(KD):
                            last = t.matmul(bank[1 + n][:, :], mn_t[s][:, k * P:(k + 1) * P],
                                            w1[:, ds(w + (k * F + n * 512), 512)], start=k == 0, stop=k == KD - 1)
                        last.then_inc(m_h[m], 1)

                def turn_hidden(i, first=False):
                    for n in range(2):
                        pe.wait_ge(m_hk[m], i * 2 + n + 1)
                        if not first:
                            pe.wait_ge(m_a[m], i)
                        for j in range(4):
                            last = t.transpose(bank[3 + n][:, j * P:(j + 1) * P],
                                               hid[:, (4 * n + j) * P:(4 * n + j + 1) * P], ident[:, :])
                        last.then_inc(m_ht[m], 1)

                def expert_out(i, s, w, first=False):
                    pe.wait_ge(m_a[m], i + 1)
                    if not first:
                        pe.wait_ge(m_r[m], i)
                    for c in range(FC):
                        last = t.matmul(bank[5][:, 0:D], act_t[s][:, c * P:(c + 1) * P],
                                        w2[:, ds(w + c * D, D)], start=c == 0, stop=c == FC - 1)
                    last.then_inc(m_y[m], 1)

                def step(i, s, first=False, more=True):
                    hidden(i, s, weights_of(i))
                    if more:
                        turn_input(i + 1, 1 - s)
                    expert_out(i - 1, 1 - s, weights_of(i - 1), first)
                    turn_hidden(i)

                pe.wait_ge(s_tab[0 if m == 0 else 2], 1)
                if m == 0:
                    for e in range(E):
                        pe.wait_ge(s_w[e], 32)
                turn_input(0, 0, True)
                hidden(0, 0, weights_of(0), True)
                turn_input(1, 1)
                turn_hidden(0, True)
                step(1, 1, True)
                with pe.Fori(0, (SLOTS - 3) // 2) as i:
                    step(i * 2 + 2, 0)
                    step(i * 2 + 3, 1)
                step(SLOTS - 1, (SLOTS - 1) % 2, more=False)
                expert_out(SLOTS - 1, (SLOTS - 1) % 2, weights_of(SLOTS - 1))

            routing(0)
            slots(0)
            for c in range(NC):
                transposes(1, c, c == 0)
                pe.wait_ge(s_te[1], c * 4 + 4)
                if c:
                    pe.wait_ge(s_seq, c)
                for b in range(NB):
                    for k in range(KD):
                        last = t.matmul(bank[4][b * DO:(b + 1) * DO, :], down_t[:, k * DO:(k + 1) * DO],
                                        xn_t[:, b, k, :], start=k == 0, stop=k == KD - 1)
                last.then_inc(s_dn, 1)

            with pe.Fori(0, NL) as l:
                pe.wait_ge(r_w, l * 3 + 3)

                def gates(c):
                    pe.wait_ge(r_xc, l * NC + c + 1)
                    if c >= 2:
                        pe.wait_ge(r_ti, l * NC + c - 1)
                    for m in range(2):
                        t.matmul(bank[2 * m + c % 2][:, :], rec_cur[:, m * P:(m + 1) * P], r_xc_b[c % 2],
                                 start=True, stop=True).then_inc(r_g, 1)

                def project(c):
                    pe.wait_ge(r_h, l * NC + c + 2)
                    if c >= 2:
                        pe.wait_ge(r_yk, l * NC + c - 1)
                    t.matmul(bank[4 + c % 2][:, :], rec_cur[:, 2 * P:3 * P], r_a_b[c],
                             start=True, stop=True).then_inc(r_y, 1)

                def norms(c):
                    pe.wait_ge(r_yk, l * NC + c + 1)
                    if c:
                        pe.wait_ge(r_sr, l * NC + c)
                    for j in range(TPC):
                        last = t.matmul(bank[7][:, j * NB:(j + 1) * NB], sq[:, j * P:(j + 1) * P], half_sel[:, :],
                                        start=True, stop=True)
                    last.then_inc(r_ss, 1)
                    pe.wait_ge(r_si, l * NC + c + 1)
                    if c:
                        pe.wait_ge(r_xx, l * NC + c + 1)
                    for j in range(TPC):
                        last = t.transpose(bank[6][:, j * P:(j + 1) * P], rms_w[:, j * P:(j + 1) * P], ident[:, :])
                    last.then_inc(r_rb, 1)

                for c in range(NC):
                    gates(c)
                project(0)
                for c in range(NC):
                    if c + 1 < NC:
                        project(c + 1)
                    norms(c)
            routing(2)
            slots(1)


_INS = ["L0_attn_h", "L0_attn_down_w", "L0_attn_up_w", "L0_attn_conv_w", "L0_attn_conv_b", "L0_attn_Wr_w",
        "L0_attn_Wr_b", "L0_attn_Wi_w", "L0_attn_Wi_b", "L0_attn_log_a", "L0_attn_out_w", "L0_attn_norm_w",
        "L0_ffn_Wr", "L0_ffn_br", "L0_ffn_ln_g", "L0_ffn_ln_b", "L0_ffn_W1", "L0_ffn_b1", "L0_ffn_W2", "L0_ffn_b2"]


def kernel(**inputs):
    import numpy as _np
    import concourse.bacc as _bacc
    from concourse import mybir as _mybir
    from concourse.bass_utils import run_bass_kernel_spmd as _run

    nc = _bacc.Bacc("TRN2", target_bir_lowering=False, num_devices=1)
    arrays, args = {}, []
    for name in _INS:
        a = _np.ascontiguousarray(inputs[name])
        arrays[f"in_{name}"] = a
        args.append(nc.dram_tensor(f"in_{name}", a.shape, _mybir.dt.from_np(a.dtype), kind="ExternalInput").ap())
    x = arrays["in_L0_attn_h"]
    args.append(nc.dram_tensor("out_x", x.shape, _mybir.dt.from_np(x.dtype), kind="ExternalOutput").ap())
    macaron_block(nc, *args)
    return _run(nc, [arrays], core_ids=[0]).results[0]["out_x"]
```

```python
from contextlib import ExitStack

import concourse.bass as bass
from concourse import mybir

ALU = mybir.AluOpType
ACT = mybir.ActivationFunctionType
F32 = mybir.dt.float32
BF16 = mybir.dt.bfloat16
I32 = mybir.dt.int32
AX = mybir.AxisListType
ds = bass.ds

P = 128
LN_EPS = 1e-5
RMS_EPS = 1e-6
LOG1P_TERMS = 8


def macaron_block(nc, h, down_w, up_w, conv_w, conv_b, gate_r_w, gate_r_b, gate_i_w, gate_i_b, log_a, out_w, norm_w,
                  router_w, router_b, ln_g, ln_b, w1_in, b1_in, w2_in, b2_in, out):
    NB, L, D = h.shape
    NT = NB * L // P
    NC = 4
    TPC = L // NC // P
    CH = L // NC
    KD = D // P
    E = router_w.shape[1]
    F = w1_in.shape[2]
    FC = F // P
    NL, DO = conv_b.shape
    T = NB * L
    REGION = T + P
    SLOTS = (T + E * (P - 1)) // P
    WE = KD * F
    C_MEAN, C_RS, C_GATE, C_ID = D, D + 1, D + 2, D + 3
    RW = D + 4
    RING = 4
    assert NB * DO == P and CH == 512 and FC * D == WE and F == 1024

    x_in = h.rearrange("b l d -> (b l) d")
    x_out = out.rearrange("b l d -> (b l) d")
    routed = nc.dram_tensor("routed_rows", [E * REGION + P, RW], F32, kind="Internal").ap()
    x_mid = nc.dram_tensor("x_after_first_ffn", [T, D], F32, kind="Internal").ap()

    with ExitStack() as ctx:
        def sb(name, shape, dt=F32):
            return ctx.enter_context(nc.sbuf_tensor(name, shape, dt))

        def sem(name):
            return ctx.enter_context(nc.semaphore(name))

        def sems(name, n):
            return [sem(f"{name}{i}") for i in range(n)]

        bank = [ctx.enter_context(nc.psum_tensor(f"bank{i}", [P, 512], F32)) for i in range(8)]

        w1 = sb("w1", [P, E * WE])
        w2 = sb("w2", [P, E * WE])
        rows = sb("rows", [P, NT * RW])
        rows_t = rows[:, :].rearrange("p (t w) -> p t w", w=RW)
        rows_bcj = rows[:, :].rearrange("p (b c j w) -> p b c j w", b=NB, c=NC, j=TPC)
        ident = sb("ident", [P, P])
        wr = sb("wr", [P, KD * E])
        down_t = sb("down_t", [P, KD * DO])
        up_t = sb("up_t", [P, D])
        rec_t = sb("rec_t", [P, 3 * NL * P])
        rec_cur = sb("rec_cur", [P, 3 * P])
        NV = E * FC + 2 * KD + 5 * NL
        vec = sb("vec", [P, NV])
        V_G, V_B = E * FC, E * FC + KD
        V_CB, V_RB, V_IB, V_LA, V_NW = (E * FC + 2 * KD + i * NL for i in range(5))
        U_CB, U_RB, U_IB, U_LS, U_NW, NU = 4, 5, 6, 7, 8, 9
        lay = sb("lay", [P, NL * NU])
        lay_l = lay[:, :].rearrange("p (l u) -> p l u", u=NU)
        cur = sb("cur", [P, NU])
        b2_seq = sb("b2_seq", [P, 3 + L])
        b2_all = b2_seq[:, 0:E * D]
        seq = b2_seq
        rb_all = sb("rb_all", [P, E])
        tri = sb("tri", [P, P], BF16)
        ones = sb("ones", [P, P], BF16)
        half_sel = sb("half_sel", [P, NB])
        e_desc = sb("e_desc", [P, E])
        e_base = sb("e_base", [P, E])
        e_fill = sb("e_fill", [P, E])
        slot_no = sb("slot_no", [P, SLOTS])
        eps_rms = sb("eps_rms", [P, 1])
        quarter = sb("quarter", [P, 1])
        fill = sb("fill", [P, RW])
        minus_half = sb("minus_half", [P, 2 * NB * TPC])
        NJ = NB * TPC
        st = sb("st", [P, NJ * 6])
        mv = [sb(f"mv{i}", [P, NJ * 2]) for i in range(2)]
        var_eps = sb("var_eps", [P, 2 * NJ])
        inv_std = [sb(f"inv_std{i}", [P, 2 * NJ]) for i in range(2)]
        lgt = sb("lgt", [P, NJ * E])
        top = sb("top", [P, NJ])
        hit = sb("hit", [P, NJ * E])
        below = sb("below", [P, NJ * E])
        expo = sb("expo", [P, NJ * E])
        first = sb("first", [P, NJ])
        onehot = sb("onehot", [P, NJ * E], BF16)
        seen = sb("seen", [P, E], BF16)
        group_sum = sb("group_sum", [P, E])
        rank = sb("rank", [P, NJ * E])
        dest_f = sb("dest_f", [P, NJ])
        dest = sb("dest", [P, NT], I32)
        den = sb("den", [P, NJ])
        cnt = sb("cnt", [P, E])
        cnt_i = sb("cnt_i", [P, 2 * E], I32)
        tiles_of = sb("tiles_of", [P, E])
        tile_end = sb("tile_end", [P, E])
        skip = sb("skip", [P, E])
        zero_e = sb("zero_e", [P, E])
        slot_e = sb("slot_e", [P, SLOTS])
        slot_r = sb("slot_r", [P, SLOTS])
        tab_fill = sb("tab_fill", [P, E], I32)
        tab_row = sb("tab_row", [P, SLOTS], I32)
        tab_w = sb("tab_w", [P, SLOTS], I32)
        tab_b = sb("tab_b", [P, SLOTS], I32)
        WORK = 12 * CH
        work = sb("work", [P, WORK])
        vec_rows = work[0:NV, WORK - P:WORK]
        past = work[:, 0:SLOTS * E]
        jump = work[:, SLOTS * E:2 * SLOTS * E]
        xn = work[:, 0:NJ * D].rearrange("p (j d) -> p j d", d=D)
        xn_t = work[:, NJ * D:NJ * D + NB * KD * CH].rearrange("p (b k t) -> p b k t", b=NB, k=KD)

        def at(pos, n):
            return work[:, pos:pos + n]

        pay = [at(i * RW, RW) for i in range(RING)]
        q = RING * RW
        mn = [at(q + i * D, D) for i in range(2)]
        q += 2 * D
        mn_t = [at(q + i * D, D) for i in range(2)]
        q += 2 * D
        hid = at(q, F)
        q += F
        act_t = [at(q + i * F, F) for i in range(2)]
        q += 2 * F
        y_b = at(q, D)
        q += D
        res = [at(q + i * D, D) for i in range(2)]
        q += 2 * D
        assert q <= WORK
        r_x_b = [at(i * CH, CH) for i in range(NC)]
        r_a_b = [at((4 + i) * CH, CH) for i in range(NC)]
        r_ti_b = [at((8 + i) * CH, CH) for i in range(NC)]
        up_x = at(8 * CH, CH)
        rms_s = sb("rms_s", [P, NC * TPC * NB])
        rms_i = sb("rms_i", [P, NC * TPC * NB])

        s_par = sem("params_loaded")
        s_x = [sems("x_loaded", NT // TPC), sems("x_mid_loaded", NT // TPC)]
        s_w = sems("expert_loaded", E)
        s_c1 = sem("pool_consts")
        s_c2 = sem("consts_ready")
        s_zero = sem("weights_zeroed")
        s_tp = sem("param_transposed")
        s_tpe = sem("param_kept")
        s_absla = sem("abs_log_a")
        s_expla = sem("exp_log_a")
        s_lsd = sem("log_sigmoid_ready")
        s_mv = sems("moments", 3)
        s_pow = sems("inverse_std", 3)
        s_xn = sems("normalised", 3)
        s_tr = sems("transposed", 3)
        s_te = sems("transposed_kept", 3)
        s_lg = sems("logits", 3)
        s_ex = sems("shifted_logits", 3)
        s_exd = sems("exponentials", 3)
        s_oh = sems("onehot_ready", 3)
        s_rk = sems("rank_ready", 3)
        s_ds = sems("rows_complete", 3)
        s_sc = sems("rows_routed", 3)
        s_seen = sems("seen_final", 3)
        s_cnt = sems("counts_ready", 3)
        s_tab = sems("tables_ready", 3)
        s_fill = sems("regions_filled", 3)
        s_b2 = sem("biases_again")
        s_dn = sem("down_projected")
        s_seq = sem("down_kept")
        s_upx = sem("up_input_staged")
        s_up = sem("up_projected")
        s_add = sem("recurrence_added")
        m_pay = [sems(f"slot_rows{m}_", RING) for m in range(2)]
        m_xn = sems("slot_normalised", 2)
        m_xt = sems("slot_transposed", 2)
        m_xk = sems("slot_affine", 2)
        m_h = sems("hidden_half", 2)
        m_hk = sems("hidden_kept", 2)
        m_ht = sems("hidden_transposed", 2)
        m_a = sems("activated", 2)
        m_y = sems("expert_out", 2)
        m_r = sems("result_ready", 2)
        m_go = sems("stores_begun", 2)
        m_s = [sems(f"result_stored{m}_", RING) for m in range(2)]
        r_w = sem("layer_weights")
        r_c0 = sem("conv_tap3")
        r_xc = sem("conv_done")
        r_g = sem("gates_projected")
        r_ti = sem("gates_activated")
        r_in = sem("input_gated")
        r_aa = sem("decay_squared")
        r_q = sem("gate_square_ready")
        r_gt = sem("input_gate_ready")
        r_h = sem("state_scanned")
        r_y = sem("out_projected")
        r_yk = sem("out_squared")
        r_ss = sem("sum_squares")
        r_sr = sem("rms_root")
        r_si = sem("rms_inverse")
        r_rb = sem("rms_spread")
        r_xx = sem("layer_output")

        N_PAR = 27

        block = ctx.enter_context(nc.Block())

        def tile_of(c, b, j, lo, n):
            return rows[:, ds(c * (TPC * RW) + (b * NC * TPC + j) * RW + lo, n)]

        def column_of(c, col):
            return rows_bcj[:, :, ds(c, 1), :, col:col + 1].rearrange("p b o j w -> p b (o j w)")

        @block.sync
        def _(sp):
            for b in range(NB):
                sp.dma_start(rows_t[:, b * NC * TPC:b * NC * TPC + TPC, 0:D],
                             x_in[b * L:b * L + CH, :].rearrange("(j p) d -> p j d", p=P)).then_inc(s_x[0][b], 16)
            sp.dma_start(wr[:, :].rearrange("p (k e) -> p k e", k=KD),
                         router_w.rearrange("(k p) e -> p k e", p=P)).then_inc(s_par, 16)
            sp.dma_start(rb_all[:, :], router_b[None, :].to_broadcast([P, E])).then_inc(s_par, 16)
            for c in range(1, NC):
                for b in range(NB):
                    t0 = (b * NC + c) * TPC
                    sp.dma_start(rows_t[:, t0:t0 + TPC, 0:D],
                                 x_in[t0 * P:(t0 + TPC) * P, :].rearrange("(j p) d -> p j d", p=P)
                                 ).then_inc(s_x[0][c * NB + b], 16)
            sp.wait_ge(s_par, 16 * N_PAR)
            for e in range(E):
                sp.dma_start(w1[:, e * WE:(e + 1) * WE].rearrange("p (k f) -> p k f", k=KD),
                             w1_in[e].rearrange("(k p) f -> p k f", p=P)).then_inc(s_w[e], 16)
                sp.dma_start(w2[:, e * WE:(e + 1) * WE].rearrange("p (c d) -> p c d", c=FC),
                             w2_in[e].rearrange("(c p) d -> p c d", p=P)).then_inc(s_w[e], 16)
            sp.wait_ge(s_c2, 1)
            sp.dma_start(routed[E * REGION:E * REGION + P, :], fill[:, :]).then_inc(s_fill[0], 16)

            def feed_slots(m, phase):
                sp.wait_ge(s_tab[phase], 1)
                for e in range(E):
                    row = sp.value_load(tab_fill[0:1, e:e + 1], min_val=0, max_val=E * REGION - P)
                    sp.dma_start(routed[ds(row, P), :], fill[:, :]).then_inc(s_fill[phase], 16)
                sp.wait_ge(s_fill[phase], 16 * (E + (phase == 0)))
                sp.wait_ge(s_sc[phase], 16 * NT)

                def slot(t, i, s, reuse):
                    row = sp.value_load(tab_row[0:1, ds(t, 1)], min_val=0, max_val=E * REGION)
                    if reuse:
                        sp.wait_ge(m_s[m][s], i * 16)
                    sp.dma_start(pay[s], routed[ds(row, P), :]).then_inc(m_pay[m][s], 16)

                for s in range(RING):
                    slot(s, 0, s, False)
                with sp.Fori(1, SLOTS // RING) as i:
                    for s in range(RING):
                        slot(i * RING + s, i, s, True)
                for s in range(SLOTS % RING):
                    slot(SLOTS // RING * RING + s, SLOTS // RING, s, True)

            feed_slots(0, 0)
            for s in range(RING):
                sp.wait_ge(m_s[0][s], 16 * ((SLOTS - s + RING - 1) // RING))
            for c in range(NC):
                for b in range(NB):
                    t0 = (b * NC + c) * TPC
                    sp.dma_start(rows_t[:, t0:t0 + TPC, 0:D],
                                 x_mid[t0 * P:(t0 + TPC) * P, :].rearrange("(j p) d -> p j d", p=P)
                                 ).then_inc(s_x[1][c * NB + b], 16)
            sp.wait_ge(s_upx, NC)
            sp.dma_start(b2_all, b2_in.rearrange("e d -> (e d)")[None, :].to_broadcast([P, E * D])).then_inc(s_b2, 16)
            feed_slots(1, 2)
            for s in range(RING):
                sp.wait_ge(m_s[1][s], 16 * ((SLOTS - s + RING - 1) // RING))

        @block.gpsimd
        def _(pool):
            g = nc.gpsimd
            g.memset(ident[:, :], 0.0)
            g.memset(rec_t[:, 0:P], 1.0)
            g.memset(rec_t[:, P:2 * P], 1.0)
            g.iota(tab_w[:, 0:SLOTS], [[1, SLOTS]], base=0, channel_multiplier=0)
            g.iota(cnt_i[:, 0:E], [[-1, E]], base=E, channel_multiplier=0)
            g.iota(tab_fill[:, :], [[REGION, E]], base=0, channel_multiplier=0)
            g.iota(cnt_i[:, E:2 * E], [[REGION, E]], base=0, channel_multiplier=1)
            g.iota(rows_t[:, :, C_ID:C_ID + 1].bitcast(I32).rearrange("p t w -> p (t w)"), [[P, NT]], base=0,
                   channel_multiplier=1)
            g.memset(fill[:, 0:C_ID], 0.0)
            g.iota(fill[:, C_ID:C_ID + 1].bitcast(I32), [[0, 1]], base=T, channel_multiplier=1)
            g.memset(minus_half[:, :], -0.5)
            g.memset(eps_rms[:, :], RMS_EPS)
            g.memset(quarter[:, :], 0.25)
            g.memset(zero_e[:, :], 0.0)
            g.memset(half_sel[:, :], 0.0)
            pool.drain()
            for b in range(NB):
                g.memset(half_sel[b * DO:(b + 1) * DO, b:b + 1], 1.0)
                pool.drain()
            g.affine_select(out=ident[:, :], in_=ident[:, :], compare_op=ALU.not_equal, fill=1.0, base=0,
                            pattern=[[-1, P]], channel_multiplier=1)
            g.affine_select(out=rec_t[:, 0:P], in_=rec_t[:, 0:P], compare_op=ALU.is_ge, fill=0.0, base=-1,
                            pattern=[[1, P]], channel_multiplier=-1).then_inc(s_c1, 1)

            def powers(phase, c):
                pool.wait_ge(s_mv[phase], c + 1)
                if c:
                    pool.drain()
                v = mv[c % 2][:, :].rearrange("p (j s) -> p j s", s=2)[:, :, 1]
                g.tensor_scalar(var_eps[:, 0:NJ], v, 1.0, LN_EPS, ALU.mult, ALU.add)
                g.tensor_scalar(var_eps[:, NJ:2 * NJ], v, 1.0 + LN_EPS, LN_EPS * LN_EPS, ALU.mult, ALU.add)
                pool.drain()
                g.tensor_tensor(inv_std[c % 2][:, :], var_eps[:, :], minus_half[:, :], ALU.pow).then_inc(s_pow[phase], 1)

            def route(phase, c):
                pool.wait_ge(s_ds[phase], c + 1)
                for b in range(NB):
                    for j in range(TPC):
                        t = (b * NC + c) * TPC + j
                        g.indirect_dma_start(
                            out=routed, out_offset=bass.IndirectOffsetOnAxis(ap=dest[:, t:t + 1], axis=0),
                            in_=rows[:, t * RW:(t + 1) * RW], in_offset=None,
                            bounds_check=E * REGION - 1, oob_is_err=False).then_inc(s_sc[phase], 16)

            def store_slots(m):
                target = x_mid if m == 0 else x_out
                last_token = pool.to_reg(T - 1)

                def slot(t, s):
                    pool.wait_ge(m_r[m], t + 1)
                    pool.sem_inc(m_go[m])
                    g.indirect_dma_start(
                        out=target, out_offset=bass.IndirectOffsetOnAxis(ap=pay[s][:, C_ID:C_ID + 1].bitcast(I32),
                                                                         axis=0),
                        in_=res[s % 2], in_offset=None, bounds_check=last_token, oob_is_err=False
                    ).then_inc(m_s[m][s], 16)

                with pool.Fori(0, SLOTS // RING) as i:
                    for s in range(RING):
                        slot(i * RING + s, s)
                for s in range(SLOTS % RING):
                    slot(SLOTS // RING * RING + s, s)

            powers(0, 0)
            powers(0, 1)
            for c in range(NC):
                if c + 2 < NC:
                    powers(0, c + 2)
                route(0, c)
            store_slots(0)
            for c in range(NC):
                powers(1, c)
            with pool.Fori(0, NL) as l:
                for c in range(NC):
                    pool.wait_ge(r_ti, l * NC + c + 1)
                    pool.wait_ge(r_in, l * NC + c + 1)
                    g.tensor_tensor(r_x_b[c], r_a_b[c], r_a_b[c], ALU.mult).then_inc(r_aa, 1)
            for c in range(NC):
                pool.wait_ge(r_xx, NL * NC + c + 1)
                if c:
                    pool.wait_ge(s_up, 2 * NB * c)
                g.tensor_copy(up_x, seq[:, 3 + c * CH:3 + (c + 1) * CH]).then_inc(s_upx, 1)
                powers(2, c)
                if c >= 2:
                    route(2, c - 2)
            route(2, NC - 2)
            route(2, NC - 1)
            store_slots(1)

        @block.vector
        def _(dve):
            v = nc.vector

            v.memset(work[:, 0:3 * NL * P], 0.0).then_inc(s_zero, 1)
            dve.wait_ge(s_c1, 1)
            v.tensor_copy(tri[:, :], rec_t[:, 0:P])
            v.tensor_copy(ones[:, :], rec_t[:, P:2 * P])
            v.tensor_copy(slot_no[:, :], tab_w[:, :])
            v.tensor_copy(e_desc[:, :], cnt_i[:, 0:E])
            v.tensor_copy(e_base[:, :], tab_fill[:, :])
            v.tensor_copy(e_fill[:, :], cnt_i[:, E:2 * E]).then_inc(s_c2, 1)

            def moments(phase, c):
                dve.drain()
                for b in range(NB):
                    for j in range(TPC):
                        jj = b * TPC + j
                        v.bn_stats(st[:, jj * 6:jj * 6 + 6], tile_of(c, b, j, 0, D))
                dve.drain()
                for jj in range(NJ):
                    last = v.bn_aggr(mv[c % 2][:, jj * 2:jj * 2 + 2], st[:, jj * 6:jj * 6 + 6])
                last.then_inc(s_mv[phase], 1)

            def normalise(phase, c):
                dve.wait_ge(s_pow[phase], c + 1)
                if c:
                    dve.wait_ge(s_tr[phase], c * 4)
                m, r = mv[c % 2], inv_std[c % 2]
                for b in range(NB):
                    for j in range(TPC):
                        jj = b * TPC + j
                        v.tensor_scalar(xn[:, jj, :], tile_of(c, b, j, 0, D), m[:, 2 * jj:2 * jj + 1],
                                        r[:, jj:jj + 1], ALU.subtract, ALU.mult)
                v.tensor_copy(column_of(c, C_MEAN), m[:, :].rearrange("p (b j s) -> p b j s", b=NB, s=2)[:, :, :, 0])
                v.tensor_copy(column_of(c, C_RS), r[:, NJ:2 * NJ].rearrange("p (b j) -> p b j", b=NB)
                              ).then_inc(s_xn[phase], 1)

            def jx(a):
                return a[:, :].rearrange("p (j e) -> p j e", e=E)

            def per_e(a):
                return a[:, None, :].to_broadcast([P, NJ, E])

            def per_j(a):
                return a[:, :, None].to_broadcast([P, NJ, E])

            def choose(phase, c):
                dve.wait_ge(s_lg[phase], c + 1)
                v.tensor_tensor(jx(lgt), bank[4 + c % 2][:, 0:NJ * E].rearrange("p (j e) -> p j e", e=E), per_e(rb_all), ALU.add)
                dve.drain()
                v.tensor_reduce(top[:, :], jx(lgt), AX.X, ALU.max)
                dve.drain()
                v.tensor_tensor(jx(below), jx(lgt), per_j(top), ALU.subtract).then_inc(s_ex[phase], 1)
                v.tensor_tensor(jx(hit), jx(lgt), per_j(top), ALU.is_equal)
                dve.drain()
                v.tensor_tensor(jx(hit), jx(hit), per_e(e_desc), ALU.mult)
                dve.drain()
                v.tensor_reduce(first[:, :], jx(hit), AX.X, ALU.max)
                dve.drain()
                v.tensor_tensor(jx(onehot), per_j(first), per_e(e_desc), ALU.is_equal).then_inc(s_oh[phase], 1)
                dve.wait_ge(s_exd[phase], c + 1)
                v.tensor_reduce(den[:, :], jx(expo), AX.X, ALU.add)
                dve.drain()
                v.tensor_reduce(group_sum[:, :], onehot[:, :].rearrange("p (j e) -> p e j", e=E), AX.X, ALU.add)
                v.reciprocal(top[:, :], den[:, :])
                dve.drain()
                v.tensor_scalar(column_of(c, C_GATE), top[:, :].rearrange("p (b j) -> p b j", b=NB), 0.5, None, ALU.mult)
                dve.wait_ge(s_rk[phase], c + 1)
                v.tensor_tensor(seen[:, :], seen[:, :], group_sum[:, :], ALU.add)
                v.tensor_tensor(jx(rank), bank[4 + c % 2][:, NJ * E:2 * NJ * E].rearrange("p (j e) -> p j e", e=E), per_e(e_base), ALU.add)
                dve.drain()
                v.tensor_tensor(jx(rank), jx(rank), jx(onehot), ALU.mult)
                dve.drain()
                v.tensor_reduce(dest_f[:, :], jx(rank), AX.X, ALU.add)
                dve.drain()
                d = dest[:, :].rearrange("p (b c j) -> p b c j", b=NB, c=NC)[:, :, ds(c, 1), :].rearrange(
                    "p b o j -> p b (o j)")
                v.tensor_copy(d, dest_f[:, :].rearrange("p (b j) -> p b j", b=NB)).then_inc(s_ds[phase], 1)

            def tables(phase):
                dve.wait_ge(s_cnt[phase], 1)
                v.tensor_copy(cnt[:, :], bank[6][:, 0:E])
                v.tensor_scalar(cnt_i[:, 0:E], bank[6][:, 0:E], float(P - 1), None, ALU.add)
                dve.drain()
                v.tensor_tensor(tab_fill[:, :], cnt[:, :], e_base[:, :], ALU.add)
                v.tensor_scalar(cnt_i[:, E:2 * E], cnt_i[:, 0:E], P.bit_length() - 1, None, ALU.logical_shift_right)
                dve.drain()
                v.tensor_copy(tiles_of[:, :], cnt_i[:, E:2 * E])
                dve.drain()
                v.tensor_tensor_scan(tile_end[:, :], tiles_of[:, :], zero_e[:, :], 0.0, ALU.add, ALU.add)
                v.tensor_scalar(skip[:, :], tiles_of[:, :], -float(P), float(REGION), ALU.mult, ALU.add)
                dve.drain()
                ps = past.rearrange("p (t e) -> p t e", e=E)
                jp = jump.rearrange("p (t e) -> p t e", e=E)
                v.tensor_tensor(ps, slot_no[:, :, None].to_broadcast([P, SLOTS, E]),
                                tile_end[:, None, :].to_broadcast([P, SLOTS, E]), ALU.is_ge)
                dve.drain()
                v.tensor_reduce(slot_e[:, :], ps, AX.X, ALU.add)
                v.tensor_tensor(jp, ps, skip[:, None, :].to_broadcast([P, SLOTS, E]), ALU.mult)
                dve.drain()
                v.tensor_reduce(slot_r[:, :], jp, AX.X, ALU.add)
                v.tensor_scalar(slot_e[:, :], slot_e[:, :], float(E - 1), float(WE), ALU.min, ALU.mult)
                dve.drain()
                v.scalar_tensor_tensor(out=slot_r[:, :], in0=slot_no[:, :], scalar=float(P), in1=slot_r[:, :],
                                       op0=ALU.mult, op1=ALU.add)
                v.tensor_copy(tab_w[:, :], slot_e[:, :])
                v.tensor_scalar(tab_b[:, :], slot_e[:, :], float(FC) / WE, None, ALU.mult)
                dve.drain()
                v.tensor_scalar(tab_row[:, :], slot_r[:, :], float(E * REGION), None, ALU.min).then_inc(s_tab[phase], 1)
                dve.drain()

            def routing(phase, before):
                v.memset(seen[:, :], 0.0)
                before(0)
                moments(phase, 0)
                before(1)
                moments(phase, 1)
                normalise(phase, 0)
                for c in range(NC):
                    if c + 2 < NC:
                        before(c + 2)
                        moments(phase, c + 2)
                    if c + 1 < NC:
                        normalise(phase, c + 1)
                    choose(phase, c)
                dve.drain()
                v.tensor_copy(top[:, 0:1], dest_f[:, 0:1]).then_inc(s_seen[phase], 1)
                tables(phase)

            def slots(m):
                def norm(t, i, s):
                    dve.wait_ge(m_pay[m][s], i * 16 + 16)
                    p = pay[s]
                    v.tensor_scalar(mn[s % 2], p[:, 0:D], p[:, C_MEAN:C_MEAN + 1], p[:, C_RS:C_RS + 1],
                                    ALU.subtract, ALU.mult).then_inc(m_xn[m], 1)

                def activate(t, s):
                    eb = dve.value_load(tab_b[0:1, ds(t, 1)], min_val=0, max_val=(E - 1) * FC)
                    for c in range(FC):
                        if c % 4 == 0:
                            dve.wait_ge(m_ht[m], t * 2 + c // 4 + 1)
                        last = v.tensor_scalar(act_t[s % 2][:, c * P:(c + 1) * P],
                                               bank[3 + c // 4][:, c % 4 * P:(c % 4 + 1) * P],
                                               vec[:, ds(eb + c, 1)], 0.0, ALU.add, ALU.max)
                    last.then_inc(m_a[m], 1)

                def finish(t, s, stored):
                    eb = dve.value_load(tab_b[0:1, ds(t, 1)], min_val=0, max_val=(E - 1) * FC)
                    dve.wait_ge(m_y[m], t + 1)
                    v.tensor_tensor(y_b, bank[5][:, 0:D], b2_all[:, ds(eb * (D // FC), D)], ALU.add)
                    dve.drain()
                    if stored is not None:
                        dve.wait_ge(m_s[m][(s + 2) % RING], stored)
                    v.scalar_tensor_tensor(out=res[s % 2], in0=y_b, scalar=pay[s][:, C_GATE:C_GATE + 1],
                                           in1=pay[s][:, 0:D], op0=ALU.mult, op1=ALU.add).then_inc(m_r[m], 1)

                def step(t, i, s, more=True, stored=True):
                    if more:
                        norm(t + 1, i + (s + 1) // RING, (s + 1) % RING)
                    sp_, ip = (s - 1) % RING, i - (s == 0)
                    finish(t - 1, sp_, (ip * 16 + 16 if sp_ >= 2 else ip * 16) if stored else None)
                    activate(t, s)

                if m == 1:
                    dve.wait_ge(s_b2, 16)
                norm(0, 0, 0)
                norm(1, 0, 1)
                activate(0, 0)
                step(1, 0, 1, stored=False)
                step(2, 0, 2, stored=False)
                step(3, 0, 3)
                with dve.Fori(1, SLOTS // RING) as i:
                    for s in range(RING):
                        step(i * RING + s, i, s)
                n = SLOTS // RING
                for s in range(SLOTS % RING):
                    step(n * RING + s, n, s, more=s < SLOTS % RING - 1)
                t = SLOTS - 1
                finish(t, t % RING, (t - 2) // RING * 16 + 16)

            def x_arrives(c):
                for b in range(NB):
                    dve.wait_ge(s_x[0][c * NB + b], 16)

            dve.wait_ge(s_tpe, 1)
            la = vec[:, V_LA:V_LA + NL]
            a0, a1, a2, a3 = (hit[:, 8 * i:8 * i + NL] for i in range(4))
            v.tensor_copy(lay_l[:, :, U_CB], vec[:, V_CB:V_CB + NL])
            v.tensor_copy(lay_l[:, :, U_NW], vec[:, V_NW:V_NW + NL])
            v.tensor_scalar(lay_l[:, :, U_RB], vec[:, V_RB:V_RB + NL], 0.5, None, ALU.mult)
            v.tensor_scalar(lay_l[:, :, U_IB], vec[:, V_IB:V_IB + NL], 0.5, None, ALU.mult)
            v.scalar_tensor_tensor(out=a0, in0=la, scalar=-1.0, in1=la, op0=ALU.mult, op1=ALU.max).then_inc(s_absla, 1)
            dve.wait_ge(s_expla, 1)
            v.tensor_scalar(a2, a1, 2.0, None, ALU.add)
            dve.drain()
            v.reciprocal(a3, a2)
            dve.drain()
            v.tensor_tensor(a1, a1, a3, ALU.mult)
            dve.drain()
            v.tensor_tensor(a2, a1, a1, ALU.mult)
            dve.drain()
            v.tensor_scalar(a3, a2, 1.0 / (2 * LOG1P_TERMS + 1), None, ALU.mult)
            for k in range(LOG1P_TERMS - 1, 0, -1):
                dve.drain()
                v.scalar_tensor_tensor(out=a3, in0=a3, scalar=1.0 / (2 * k + 1), in1=a2, op0=ALU.add, op1=ALU.mult)
            dve.drain()
            v.scalar_tensor_tensor(out=a3, in0=a3, scalar=1.0, in1=a1, op0=ALU.add, op1=ALU.mult)
            v.tensor_scalar(a0, la, 0.0, 4.0, ALU.min, ALU.mult)
            dve.drain()
            v.scalar_tensor_tensor(out=lay_l[:, :, U_LS], in0=a3, scalar=-8.0, in1=a0, op0=ALU.mult, op1=ALU.add
                                   ).then_inc(s_lsd, 1)

            dve.wait_ge(s_par, 16 * N_PAR)
            routing(0, x_arrives)
            slots(0)

            def mid_arrives(c):
                for b in range(NB):
                    dve.wait_ge(s_x[1][c * NB + b], 16)

            mid_arrives(0)
            moments(1, 0)
            for c in range(NC):
                if c + 1 < NC:
                    mid_arrives(c + 1)
                    moments(1, c + 1)
                normalise(1, c)

            dve.wait_ge(s_seq, NC)
            v.memset(seq[:, 0:3], 0.0).then_inc(r_xx, NC)
            v.memset(rms_i[:, :], 0.0).then_inc(r_h, 1)
            dve.drain()

            def convolve(l, c):
                xc = r_x_b[c]
                dve.wait_ge(r_c0, l * NC + c + 1)
                for k in range(2, -1, -1):
                    last = v.scalar_tensor_tensor(out=xc, in0=seq[:, c * CH + k:c * CH + k + CH],
                                                  scalar=cur[:, k:k + 1], in1=xc, op0=ALU.mult, op1=ALU.add)
                    if k:
                        dve.drain()
                last.then_inc(r_xc, 1)

            def gate_input(l, c):
                dve.wait_ge(r_ti, l * NC + c + 1)
                v.scalar_tensor_tensor(out=r_ti_b[c], in0=r_ti_b[c], scalar=1.0, in1=r_x_b[c],
                                       op0=ALU.add, op1=ALU.mult).then_inc(r_in, 1)

            def clamp(l, c):
                dve.wait_ge(r_aa, l * NC + c + 1)
                v.tensor_scalar(r_x_b[c], r_x_b[c], 1.0, None, ALU.min).then_inc(r_q, 1)

            def scan(l, c):
                dve.wait_ge(r_gt, l * NC + c + 1)
                v.tensor_tensor(r_x_b[c], r_x_b[c], r_ti_b[c], ALU.mult)
                dve.drain()
                prev = 0.0 if c == 0 else r_a_b[c - 1][:, CH - 1:CH]
                v.tensor_tensor_scan(r_a_b[c], r_a_b[c], r_x_b[c], prev, ALU.mult, ALU.add).then_inc(r_h, 1)

            def inverse(l):
                dve.wait_ge(r_sr, l + 1)
                v.reciprocal(rms_i[:, :], rms_s[:, :])
                dve.drain()
                for c in range(NC):
                    v.tensor_copy(r_a_b[c].rearrange("p (g n) -> p g n", n=DO),
                                  rms_i[:, c * TPC * NB:(c + 1) * TPC * NB, None].to_broadcast([P, TPC * NB, DO])
                                  ).then_inc(r_si, 1)

            def rescale(l, c):
                dve.wait_ge(r_rb, l * NC + c + 1)
                v.tensor_tensor(seq[:, 3 + c * CH:3 + (c + 1) * CH], r_ti_b[c], bank[c][:, :], ALU.mult
                                ).then_inc(r_xx, 1)

            with dve.Fori(0, NL) as l:
                convolve(l, 0)
                for c in range(NC):
                    if c + 1 < NC:
                        convolve(l, c + 1)
                    gate_input(l, c)
                clamp(l, 0)
                for c in range(NC):
                    if c + 1 < NC:
                        clamp(l, c + 1)
                    scan(l, c)
                inverse(l)
                for c in range(NC):
                    rescale(l, c)
                dve.drain()

            def recurrence_arrives(c):
                for b in range(NB):
                    for hh in range(2):
                        n = (c * NB + b) * 2 + hh
                        dve.wait_ge(s_up, n + 1)
                        r = rows_t[:, (b * NC + c) * TPC + 2 * hh:(b * NC + c) * TPC + 2 * hh + 2, 0:D]
                        v.tensor_tensor(r, r, bank[7 if hh else 6][:, :].rearrange("p (j d) -> p j d", d=D), ALU.add
                                        ).then_inc(s_add, 1)
                dve.drain()

            routing(2, recurrence_arrives)
            slots(1)

        @block.scalar
        def _(act):
            a = nc.scalar
            n_par = [2]

            def load(dst, src):
                act.dma_start(dst, src).then_inc(s_par, 16)
                n_par[0] += 1

            load(vec_rows[0:E * FC, :], b1_in.rearrange("e (c p) -> (e c) p", p=P))
            load(vec_rows[V_G:V_G + KD, :], ln_g.rearrange("(k p) -> k p", p=P))
            load(vec_rows[V_B:V_B + KD, :], ln_b.rearrange("(k p) -> k p", p=P))
            for pos, src in ((V_CB, conv_b), (V_RB, gate_r_b), (V_IB, gate_i_b), (V_LA, log_a), (V_NW, norm_w)):
                for b in range(NB):
                    load(vec_rows[pos:pos + NL, b * DO:(b + 1) * DO], src)
            for b in range(NB):
                load(lay_l[b * DO:(b + 1) * DO, :, 0:4], conv_w.rearrange("l c k -> c l k"))
            load(b2_all, b2_in.rearrange("e d -> (e d)")[None, :].to_broadcast([P, E * D]))
            act.wait_ge(s_zero, 1)
            nat = work[:, 0:3 * NL * P].rearrange("p (m l i) -> p m l i", m=3, l=NL)
            for m, src in enumerate((gate_r_w, gate_i_w, out_w)):
                for b in range(NB):
                    load(nat[b * DO:(b + 1) * DO, m, :, b * DO:(b + 1) * DO], src.rearrange("l o i -> o l i"))
            load(work[0:DO, 3 * NL * P:3 * NL * P + D], down_w)
            upn = work[:, 3 * NL * P + D:3 * NL * P + 2 * D].rearrange("p (k b i) -> p k b i", k=KD, b=NB)
            for b in range(NB):
                load(upn[:, :, b, :], up_w.rearrange("(k p) i -> p k i", p=P))
            assert n_par[0] == N_PAR, n_par[0]

            act.wait_ge(s_tp, 1)
            a.activation(vec[:, :], bank[0][:, 0:NV], ACT.Copy).then_inc(s_tpe, 1)
            for m in range(3):
                a.activation(rec_t[:, m * NL * P:(m + 1) * NL * P], bank[1 + m][:, 0:NL * P], ACT.Copy)
            a.activation(down_t[:, :], bank[4][:, 0:KD * DO], ACT.Copy)
            a.activation(up_t[:, :], bank[5][:, 0:D], ACT.Copy).then_inc(s_tpe, 1)
            act.wait_ge(s_absla, 1)
            a.activation(hit[:, 8:8 + NL], hit[:, 0:NL], ACT.Exp, scale=-1.0).then_inc(s_expla, 1)

            def keep(phase, c, guard):
                for n in range(NB * KD):
                    act.wait_ge(s_tr[phase], c * 4 + n + 1)
                    if n == 0 and guard:
                        act.wait_ge(s_lg[phase] if phase != 1 else s_dn, c)
                    a.activation(xn_t[:, n // KD, n % KD, :], bank[n][:, :], ACT.Copy).then_inc(s_te[phase], 1)

            def exponentials(phase, c):
                act.wait_ge(s_ex[phase], c + 1)
                a.activation(expo[:, :], below[:, :], ACT.Exp).then_inc(s_exd[phase], 1)

            def routing(phase):
                keep(phase, 0, False)
                with act.Fori(1, NC) as c:
                    keep(phase, c, True)
                    exponentials(phase, c - 1)
                exponentials(phase, NC - 1)

            def slots(m):
                def affine(t, s):
                    act.wait_ge(m_xt[m], t + 1)
                    for k in range(KD):
                        last = a.activation(mn_t[s % 2][:, k * P:(k + 1) * P], bank[0][:, k * P:(k + 1) * P], ACT.Identity,
                                            scale=vec[:, V_G + k:V_G + k + 1], bias=vec[:, V_B + k:V_B + k + 1])
                    last.then_inc(m_xk[m], 1)

                def hidden(t):
                    for n in range(2):
                        act.wait_ge(m_h[m], t * 2 + n + 1)
                        a.activation(hid[:, n * 512:(n + 1) * 512], bank[1 + n][:, :], ACT.Copy).then_inc(m_hk[m], 1)

                affine(0, 0)
                hidden(0)
                affine(1, 1)
                with act.Fori(0, (SLOTS - 3) // 2) as i:
                    for s in range(2):
                        hidden(i * 2 + 1 + s)
                        affine(i * 2 + 2 + s, s)
                hidden(SLOTS - 2)
                affine(SLOTS - 1, (SLOTS - 1) % 2)
                hidden(SLOTS - 1)

            routing(0)
            slots(0)
            for c in range(NC):
                keep(1, c, c > 0)
                act.wait_ge(s_dn, c + 1)
                a.activation(seq[:, 3 + c * CH:3 + (c + 1) * CH], bank[4][:, :], ACT.Copy).then_inc(s_seq, 1)
            act.wait_ge(s_lsd, 1)
            act.drain()

            with act.Fori(0, NL) as l:
                for m in range(3):
                    a.activation(rec_cur[:, m * P:(m + 1) * P], rec_t[:, ds(l * P + m * NL * P, P)], ACT.Copy
                                 ).then_inc(r_w, 1)
                a.activation(cur[:, :], lay[:, ds(l * NU, NU)], ACT.Copy)
                act.drain()

                def tap(c):
                    act.wait_ge(r_xx, l * NC + c + 1)
                    a.activation(r_x_b[c], seq[:, 3 + c * CH:3 + (c + 1) * CH], ACT.Identity,
                                 scale=cur[:, 3:4], bias=cur[:, U_CB:U_CB + 1]).then_inc(r_c0, 1)

                def gates(c):
                    act.wait_ge(r_g, (l * NC + c) * 2 + 2)
                    a.activation(r_a_b[c], bank[c % 2][:, :], ACT.Tanh, scale=0.5, bias=cur[:, U_RB:U_RB + 1])
                    a.activation(r_ti_b[c], bank[2 + c % 2][:, :], ACT.Tanh, scale=0.5,
                                 bias=cur[:, U_IB:U_IB + 1])
                    act.drain()
                    a.activation(r_a_b[c], r_a_b[c], ACT.Exp, scale=cur[:, U_LS:U_LS + 1],
                                 bias=cur[:, U_LS:U_LS + 1]).then_inc(r_ti, 1)

                def root(c):
                    act.wait_ge(r_q, l * NC + c + 1)
                    a.activation(r_x_b[c], r_x_b[c], ACT.Sqrt, scale=-0.25, bias=quarter[:, :]
                                 ).then_inc(r_gt, 1)

                def squares(c):
                    act.wait_ge(r_y, l * NC + c + 1)
                    a.activation(r_ti_b[c], bank[4 + c % 3][:, :], ACT.Copy, scale=cur[:, U_NW:U_NW + 1])
                    a.activation(r_x_b[c], bank[4 + c % 3][:, :], ACT.Square).then_inc(r_yk, 1)

                tap(0)
                for c in range(NC):
                    if c + 1 < NC:
                        tap(c + 1)
                    gates(c)
                root(0)
                for c in range(NC):
                    if c + 1 < NC:
                        root(c + 1)
                    squares(c)
                act.wait_ge(r_ss, l * NC + NC)
                a.activation(rms_s[:, :], bank[7][:, 0:NC * TPC * NB], ACT.Sqrt, scale=1.0 / DO, bias=eps_rms[:, :]
                             ).then_inc(r_sr, 1)
            routing(2)
            slots(1)

        @block.tensor
        def _(pe):
            t = nc.tensor
            pe.wait_ge(s_par, 16 * N_PAR)
            pe.wait_ge(s_c2, 1)
            t.transpose(bank[0][:, 0:NV], vec_rows, ident[0:NV, 0:NV])
            for m in range(3):
                for l in range(NL):
                    t.transpose(bank[1 + m][:, l * P:(l + 1) * P], work[:, (m * NL + l) * P:(m * NL + l + 1) * P],
                                ident[:, :])
            q = 3 * NL * P
            for k in range(KD):
                t.transpose(bank[4][:, k * DO:(k + 1) * DO], work[0:DO, q + k * P:q + (k + 1) * P], ident[0:DO, 0:DO])
            for k in range(KD):
                last = t.transpose(bank[5][:, k * P:(k + 1) * P], work[:, q + D + k * P:q + D + (k + 1) * P],
                                   ident[:, :])
            last.then_inc(s_tp, 1)

            def transposes(phase, c, first):
                pe.wait_ge(s_xn[phase], c + 1)
                for b in range(NB):
                    for k in range(KD):
                        n = b * KD + k
                        if not first:
                            pe.wait_ge(s_te[phase], (c - 1) * 4 + n + 1)
                        for j in range(TPC):
                            last = t.transpose(bank[n][:, j * P:(j + 1) * P],
                                               xn[:, b * TPC + j, k * P:(k + 1) * P], ident[:, :])
                        last.then_inc(s_tr[phase], 1)

            def logits(phase, c):
                pe.wait_ge(s_te[phase], c * 4 + 4)
                if c >= 2:
                    pe.wait_ge(s_ds[phase], c - 1)
                for b in range(NB):
                    for j in range(TPC):
                        o = (b * TPC + j) * E
                        for k in range(KD):
                            last = t.matmul(bank[4 + c % 2][:, o:o + E], xn_t[:, b, k, j * P:(j + 1) * P],
                                            wr[:, k * E:(k + 1) * E], start=k == 0, stop=k == KD - 1)
                last.then_inc(s_lg[phase], 1)

            def ranks(phase, c):
                pe.wait_ge(s_oh[phase], c + 1)
                o3 = bank[4 + c % 2][:, NJ * E:2 * NJ * E]
                t.matmul(o3, tri[:, :], onehot[:, :], start=True, stop=False)
                t.matmul(o3.rearrange("p (j e) -> p j e", e=E), ones[:, :],
                         seen[:, None, :].to_broadcast([P, NJ, E]), start=False, stop=False)
                for j in range(NJ - 1):
                    last = t.matmul(o3[:, (j + 1) * E:NJ * E].rearrange("p (j e) -> p j e", e=E), ones[:, :],
                                    onehot[:, None, j * E:(j + 1) * E].to_broadcast([P, NJ - 1 - j, E]),
                                    start=False, stop=j == NJ - 2)
                last.then_inc(s_rk[phase], 1)

            def up(c):
                pe.wait_ge(s_upx, c + 1)
                for b in range(NB):
                    for hh in range(2):
                        n = (c * NB + b) * 2 + hh
                        if n >= 2:
                            pe.wait_ge(s_add, n - 1)
                        for j in range(2):
                            jj = 2 * hh + j
                            last = t.matmul(bank[7 if hh else 6][:, j * D:(j + 1) * D],
                                            up_x[b * DO:(b + 1) * DO, jj * P:(jj + 1) * P],
                                            up_t[b * DO:(b + 1) * DO, :], start=True, stop=True)
                        last.then_inc(s_up, 1)

            def routing(phase):
                if phase == 2:
                    up(0)
                    up(1)
                transposes(phase, 0, True)
                logits(phase, 0)
                for c in range(NC):
                    if phase == 2 and c + 2 < NC:
                        up(c + 2)
                    if c + 1 < NC:
                        transposes(phase, c + 1, False)
                        logits(phase, c + 1)
                    ranks(phase, c)
                pe.wait_ge(s_seen[phase], 1)
                t.matmul(bank[6][:, 0:E], ones[:, :], seen[:, :], start=True, stop=True).then_inc(s_cnt[phase], 1)

            def slots(m):
                def turn_input(i, s, first=False):
                    pe.wait_ge(m_xn[m], i + 1)
                    if not first:
                        pe.wait_ge(m_xk[m], i)
                    for k in range(KD):
                        last = t.transpose(bank[0][:, k * P:(k + 1) * P], mn[s][:, k * P:(k + 1) * P], ident[:, :])
                    last.then_inc(m_xt[m], 1)

                def weights_of(i):
                    return pe.value_load(tab_w[0:1, ds(i, 1)], min_val=0, max_val=(E - 1) * WE)

                def hidden(i, s, w, first=False):
                    pe.wait_ge(m_xk[m], i + 1)
                    for n in range(2):
                        if not first:
                            pe.wait_ge(m_hk[m], (i - 1) * 2 + n + 1)
                        for k in range(KD):
                            last = t.matmul(bank[1 + n][:, :], mn_t[s][:, k * P:(k + 1) * P],
                                            w1[:, ds(w + (k * F + n * 512), 512)], start=k == 0, stop=k == KD - 1)
                        last.then_inc(m_h[m], 1)

                def turn_hidden(i, first=False):
                    for n in range(2):
                        pe.wait_ge(m_hk[m], i * 2 + n + 1)
                        if not first:
                            pe.wait_ge(m_a[m], i)
                        for j in range(4):
                            last = t.transpose(bank[3 + n][:, j * P:(j + 1) * P],
                                               hid[:, (4 * n + j) * P:(4 * n + j + 1) * P], ident[:, :])
                        last.then_inc(m_ht[m], 1)

                def expert_out(i, s, w, first=False):
                    pe.wait_ge(m_a[m], i + 1)
                    if not first:
                        pe.wait_ge(m_r[m], i)
                    for c in range(FC):
                        last = t.matmul(bank[5][:, 0:D], act_t[s][:, c * P:(c + 1) * P],
                                        w2[:, ds(w + c * D, D)], start=c == 0, stop=c == FC - 1)
                    last.then_inc(m_y[m], 1)

                def step(i, s, first=False, more=True):
                    w, w_before = weights_of(i), weights_of(i - 1)
                    hidden(i, s, w)
                    if more:
                        turn_input(i + 1, 1 - s)
                    expert_out(i - 1, 1 - s, w_before, first)
                    turn_hidden(i)

                pe.wait_ge(s_tab[0 if m == 0 else 2], 1)
                if m == 0:
                    for e in range(E):
                        pe.wait_ge(s_w[e], 32)
                turn_input(0, 0, True)
                hidden(0, 0, weights_of(0), True)
                turn_input(1, 1)
                turn_hidden(0, True)
                step(1, 1, True)
                with pe.Fori(0, (SLOTS - 3) // 2) as i:
                    step(i * 2 + 2, 0)
                    step(i * 2 + 3, 1)
                step(SLOTS - 1, (SLOTS - 1) % 2, more=False)
                expert_out(SLOTS - 1, (SLOTS - 1) % 2, weights_of(SLOTS - 1))

            routing(0)
            slots(0)
            for c in range(NC):
                transposes(1, c, c == 0)
                pe.wait_ge(s_te[1], c * 4 + 4)
                if c:
                    pe.wait_ge(s_seq, c)
                for b in range(NB):
                    for k in range(KD):
                        last = t.matmul(bank[4][b * DO:(b + 1) * DO, :], down_t[:, k * DO:(k + 1) * DO],
                                        xn_t[:, b, k, :], start=k == 0, stop=k == KD - 1)
                last.then_inc(s_dn, 1)

            with pe.Fori(0, NL) as l:
                pe.wait_ge(r_w, l * 3 + 3)

                def gates(c):
                    pe.wait_ge(r_xc, l * NC + c + 1)
                    if c >= 2:
                        pe.wait_ge(r_ti, l * NC + c - 1)
                    for m in range(2):
                        t.matmul(bank[2 * m + c % 2][:, :], rec_cur[:, m * P:(m + 1) * P], r_x_b[c],
                                 start=True, stop=True).then_inc(r_g, 1)

                def project(c):
                    pe.wait_ge(r_h, l * NC + c + 2)
                    if c >= 3:
                        pe.wait_ge(r_yk, l * NC + c - 2)
                    t.matmul(bank[4 + c % 3][:, :], rec_cur[:, 2 * P:3 * P], r_a_b[c], start=True, stop=True
                             ).then_inc(r_y, 1)

                def norms(c):
                    pe.wait_ge(r_yk, l * NC + c + 1)
                    for j in range(TPC):
                        o = (c * TPC + j) * NB
                        last = t.matmul(bank[7][:, o:o + NB], r_x_b[c][:, j * P:(j + 1) * P], half_sel[:, :],
                                        start=True, stop=True)
                    last.then_inc(r_ss, 1)

                def spread(c):
                    pe.wait_ge(r_si, l * NC + c + 1)
                    for j in range(TPC):
                        last = t.transpose(bank[c][:, j * P:(j + 1) * P], r_a_b[c][:, j * P:(j + 1) * P], ident[:, :])
                    last.then_inc(r_rb, 1)

                for c in range(NC):
                    gates(c)
                project(0)
                for c in range(NC):
                    if c + 1 < NC:
                        project(c + 1)
                    norms(c)
                for c in range(NC):
                    spread(c)
            routing(2)
            slots(1)


_INS = ["L0_attn_h", "L0_attn_down_w", "L0_attn_up_w", "L0_attn_conv_w", "L0_attn_conv_b", "L0_attn_Wr_w",
        "L0_attn_Wr_b", "L0_attn_Wi_w", "L0_attn_Wi_b", "L0_attn_log_a", "L0_attn_out_w", "L0_attn_norm_w",
        "L0_ffn_Wr", "L0_ffn_br", "L0_ffn_ln_g", "L0_ffn_ln_b", "L0_ffn_W1", "L0_ffn_b1", "L0_ffn_W2", "L0_ffn_b2"]


def kernel(**inputs):
    import numpy as _np
    import concourse.bacc as _bacc
    from concourse import mybir as _mybir
    from concourse.bass_utils import run_bass_kernel_spmd as _run

    nc = _bacc.Bacc("TRN2", target_bir_lowering=False, num_devices=1)
    arrays, args = {}, []
    for name in _INS:
        a = _np.ascontiguousarray(inputs[name])
        arrays[f"in_{name}"] = a
        args.append(nc.dram_tensor(f"in_{name}", a.shape, _mybir.dt.from_np(a.dtype), kind="ExternalInput").ap())
    x = arrays["in_L0_attn_h"]
    args.append(nc.dram_tensor("out_x", x.shape, _mybir.dt.from_np(x.dtype), kind="ExternalOutput").ap())
    macaron_block(nc, *args)
    return _run(nc, [arrays], core_ids=[0]).results[0]["out_x"]
```

```python
from contextlib import ExitStack

import concourse.bass as bass
from concourse import mybir

ALU = mybir.AluOpType
ACT = mybir.ActivationFunctionType
F32 = mybir.dt.float32
BF16 = mybir.dt.bfloat16
I32 = mybir.dt.int32
AX = mybir.AxisListType
ds = bass.ds

P = 128
LN_EPS = 1e-5
RMS_EPS = 1e-6
LOG1P_TERMS = 8


def macaron_block(nc, h, down_w, up_w, conv_w, conv_b, gate_r_w, gate_r_b, gate_i_w, gate_i_b, log_a, out_w, norm_w,
                  router_w, router_b, ln_g, ln_b, w1_in, b1_in, w2_in, b2_in, out):
    NB, L, D = h.shape
    NT = NB * L // P
    NC = 4
    TPC = L // NC // P
    CH = L // NC
    KD = D // P
    E = router_w.shape[1]
    F = w1_in.shape[2]
    FC = F // P
    NL, DO = conv_b.shape
    T = NB * L
    REGION = T + P
    SLOTS = (T + E * (P - 1)) // P
    WE = KD * F
    C_MEAN, C_RS, C_GATE, C_ID = D, D + 1, D + 2, D + 3
    RW = D + 4
    RING = 4
    assert NB * DO == P and CH == 512 and FC * D == WE and F == 1024

    x_in = h.rearrange("b l d -> (b l) d")
    x_out = out.rearrange("b l d -> (b l) d")
    routed = nc.dram_tensor("routed_rows", [E * REGION + P, RW], F32, kind="Internal").ap()
    x_mid = nc.dram_tensor("x_after_first_ffn", [T, D], F32, kind="Internal").ap()

    with ExitStack() as ctx:
        def sb(name, shape, dt=F32):
            return ctx.enter_context(nc.sbuf_tensor(name, shape, dt))

        def sem(name):
            return ctx.enter_context(nc.semaphore(name))

        def sems(name, n):
            return [sem(f"{name}{i}") for i in range(n)]

        bank = [ctx.enter_context(nc.psum_tensor(f"bank{i}", [P, 512], F32)) for i in range(8)]

        w1 = sb("w1", [P, E * WE])
        w2 = sb("w2", [P, E * WE])
        rows = sb("rows", [P, NT * RW])
        rows_t = rows[:, :].rearrange("p (t w) -> p t w", w=RW)
        rows_bcj = rows[:, :].rearrange("p (b c j w) -> p b c j w", b=NB, c=NC, j=TPC)
        ident = sb("ident", [P, P])
        wr = sb("wr", [P, KD * E])
        down_t = sb("down_t", [P, KD * DO])
        up_t = sb("up_t", [P, D])
        rec_t = sb("rec_t", [P, 3 * NL * P])
        rec_cur = sb("rec_cur", [P, 3 * P])
        NV = E * FC + 2 * KD + 5 * NL
        vec = sb("vec", [P, NV])
        V_G, V_B = E * FC, E * FC + KD
        V_CB, V_RB, V_IB, V_LA, V_NW = (E * FC + 2 * KD + i * NL for i in range(5))
        U_CB, U_RB, U_IB, U_LS, U_NW, NU = 4, 5, 6, 7, 8, 9
        lay = sb("lay", [P, NL * NU])
        lay_l = lay[:, :].rearrange("p (l u) -> p l u", u=NU)
        cur = sb("cur", [P, NU])
        b2_seq = sb("b2_seq", [P, 3 + L])
        b2_all = b2_seq[:, 0:E * D]
        seq = b2_seq
        rb_all = sb("rb_all", [P, E])
        tri = sb("tri", [P, P], BF16)
        ones = sb("ones", [P, P], BF16)
        half_sel = sb("half_sel", [P, NB])
        e_desc = sb("e_desc", [P, E])
        e_base = sb("e_base", [P, E])
        e_fill = sb("e_fill", [P, E])
        slot_no = sb("slot_no", [P, SLOTS])
        eps_rms = sb("eps_rms", [P, 1])
        quarter = sb("quarter", [P, 1])
        fill = sb("fill", [P, RW])
        minus_half = sb("minus_half", [P, 2 * NB * TPC])
        NJ = NB * TPC
        st = sb("st", [P, NJ * 6])
        mv = [sb(f"mv{i}", [P, NJ * 2]) for i in range(2)]
        var_eps = [sb(f"var_eps{i}", [P, 2 * NJ]) for i in range(2)]
        inv_std = [sb(f"inv_std{i}", [P, 2 * NJ]) for i in range(2)]
        lgt = sb("lgt", [P, NJ * E])
        top = sb("top", [P, NJ])
        hit = sb("hit", [P, NJ * E])
        below = sb("below", [P, NJ * E])
        expo = sb("expo", [P, NJ * E])
        first = sb("first", [P, NJ])
        chosen = sb("chosen", [P, E * (NJ + 1)], BF16)
        chosen_t = chosen[:, :].rearrange("p (e k) -> p e k", e=E)
        seen, onehot = chosen_t[:, :, 0:1], chosen_t[:, :, 1:NJ + 1]
        onehot_j = onehot.rearrange("p e j -> p j e")
        sums = sb("sums", [P, E * (NJ + 1)], BF16)
        sums_t = sums[:, :].rearrange("p (e k) -> p e k", e=E)
        carry = sb("carry", [P, E * (NJ + 1)])
        rank = sb("rank", [P, NJ * E])
        dest_f = sb("dest_f", [P, NJ])
        dest = sb("dest", [P, NT], I32)
        den = sb("den", [P, NJ])
        cnt = sb("cnt", [P, E])
        cnt_i = sb("cnt_i", [P, 2 * E], I32)
        tiles_of = sb("tiles_of", [P, E])
        tile_end = sb("tile_end", [P, E])
        skip = sb("skip", [P, E])
        zero_e = sb("zero_e", [P, E])
        slot_e = sb("slot_e", [P, SLOTS])
        slot_r = sb("slot_r", [P, SLOTS])
        tab_fill = sb("tab_fill", [P, E], I32)
        tab_row = sb("tab_row", [P, SLOTS], I32)
        tab_b = sb("tab_b", [P, SLOTS], I32)
        tab_used = sb("tab_used", [P, 1], I32)
        tab_stored = sb("tab_stored", [P, RING], I32)
        uses = sb("uses", [P, RING])
        uses_i = sb("uses_i", [P, RING], I32)
        WORK = 12 * CH
        work = sb("work", [P, WORK])
        RAW = NJ * D + NB * KD * CH
        vec_rows = work[0:NV, WORK - P:WORK]
        assert RAW + 3 * NL * P + 2 * D <= WORK - P
        past = work[:, 0:SLOTS * E]
        jump = work[:, SLOTS * E:2 * SLOTS * E]
        xn_a, xn_b = (work[:, o:o + NJ * D].rearrange("p (j d) -> p j d", d=D) for o in (0, RAW))
        xn = [[xn_a, xn_a], [xn_a, xn_b], [xn_a, xn_b]]
        xn_t = work[:, NJ * D:NJ * D + NB * KD * CH].rearrange("p (b k t) -> p b k t", b=NB, k=KD)

        def at(pos, n):
            return work[:, pos:pos + n]

        pay = [at(i * RW, RW) for i in range(RING)]
        q = RING * RW
        mn = [at(q + i * D, D) for i in range(2)]
        q += 2 * D
        mn_t = [at(q + i * D, D) for i in range(2)]
        q += 2 * D
        hid = at(q, F)
        q += F
        act_t = [at(q + i * F, F) for i in range(2)]
        q += 2 * F
        y_b = at(q, D)
        q += D
        res = [at(q + i * D, D) for i in range(2)]
        q += 2 * D
        assert q <= WORK
        r_x_b = [at(i * CH, CH) for i in range(NC)]
        r_a_b = [at((4 + i) * CH, CH) for i in range(NC)]
        r_ti_b = [at((8 + i) * CH, CH) for i in range(NC)]
        AHEAD = 3
        HC = NC // 2
        NH = HC * TPC * NB
        sums_of_squares = [bank[7][:, 0:NH], bank[3][:, 0:NH]]
        rms_s = sb("rms_s", [P, NC * TPC * NB])
        rms_i = sb("rms_i", [P, NC * TPC * NB])

        EARLY = E - 2
        LEAD = {0: 3, 2: 2}

        s_par = sem("params_loaded")
        s_rt = sem("router_loaded")
        s_x = [sems("x_loaded", NT // TPC), sems("x_mid_loaded", NT // TPC)]
        s_w = sems("expert_loaded", E)
        s_upto = sem("experts_loaded_up_to")
        s_c1 = sem("pool_consts")
        s_c2 = sem("consts_ready")
        s_zero = sem("weights_zeroed")
        s_tp = sem("param_transposed")
        s_tpe = sem("param_kept")
        s_absla = sem("abs_log_a")
        s_expla = sem("exp_log_a")
        s_lsd = sem("log_sigmoid_ready")
        s_mv = sems("moments", 3)
        s_pow = sems("inverse_std", 3)
        s_xn = sems("normalised", 3)
        s_tr = sems("transposed", 3)
        s_te = sems("transposed_kept", 3)
        s_lg = sems("logits", 3)
        s_ex = sems("shifted_logits", 3)
        s_exd = sems("exponentials", 3)
        s_oh = sems("onehot_ready", 3)
        s_rk = sems("rank_ready", 3)
        s_ds = sems("rows_complete", 3)
        s_sc = sems("rows_routed", 3)
        s_seen = sems("seen_final", 3)
        s_cnt = sems("counts_ready", 3)
        s_end = sems("regions_ends_ready", 3)
        s_tab = sems("tables_ready", 3)
        s_fill = sems("regions_filled", 3)
        s_b2 = sem("biases_again")
        s_dn = sem("down_projected")
        s_seq = sem("down_kept")
        s_up = sem("up_projected")
        s_add = sem("recurrence_added")
        m_pay = [sems(f"slot_rows{m}_", RING) for m in range(2)]
        m_xn = sems("slot_normalised", 2)
        m_xt = sems("slot_transposed", 2)
        m_xk = sems("slot_affine", 2)
        m_h = sems("hidden_half", 2)
        m_hk = sems("hidden_kept", 2)
        m_ht = sems("hidden_transposed", 2)
        m_a = sems("activated", 2)
        m_y = sems("expert_out", 2)
        m_r = sems("result_ready", 2)
        m_go = sems("stores_begun", 2)
        m_s = [sems(f"result_stored{m}_", RING) for m in range(2)]
        m_end = sem("slot_inputs_done")
        m_out = sems("buffers_all_stored", 2)
        r_w = sem("layer_weights")
        r_c0 = sem("conv_tap3")
        r_xc = sem("conv_done")
        r_g = sem("gates_projected")
        r_ti = sem("gates_activated")
        r_in = sem("input_gated")
        r_aa = sem("decay_squared")
        r_q = sem("gate_square_ready")
        r_gt = sem("input_gate_ready")
        r_h = sem("state_scanned")
        r_y = sem("out_projected")
        r_yk = sem("out_squared")
        r_ss = sem("sum_squares")
        r_sr = sem("rms_root")
        r_si = sem("rms_inverse")
        r_rb = sem("rms_spread")
        r_xx = sem("layer_output")

        N_PAR = 25

        block = ctx.enter_context(nc.Block())

        def tile_of(c, b, j, lo, n):
            return rows[:, ds(c * (TPC * RW) + (b * NC * TPC + j) * RW + lo, n)]

        def column_of(c, col):
            return rows_bcj[:, :, ds(c, 1), :, col:col + 1].rearrange("p b o j w -> p b (o j w)")

        def fill_regions(eng, phase, e0):
            eng.wait_ge(s_end[phase], 1)
            for e in range(e0, E, 2):
                row = eng.value_load(tab_fill[0:1, e:e + 1], min_val=0, max_val=E * REGION - P)
                eng.dma_start(routed[ds(row, P), :], fill[:, :]).then_inc(s_fill[phase], 16)

        def slots_used(eng):
            return eng.value_load(tab_used[0:1, 0:1], min_val=NT, max_val=SLOTS)

        @block.sync
        def _(sp):
            def load_parameters():
                n_par = [0]

                def load(dst, src):
                    sp.dma_start(dst, src).then_inc(s_par, 16)
                    n_par[0] += 1

                load(vec_rows[0:E * FC, :], b1_in.rearrange("e (c p) -> (e c) p", p=P))
                load(vec_rows[V_G:V_G + KD, :], ln_g.rearrange("(k p) -> k p", p=P))
                load(vec_rows[V_B:V_B + KD, :], ln_b.rearrange("(k p) -> k p", p=P))
                for pos, src in ((V_CB, conv_b), (V_RB, gate_r_b), (V_IB, gate_i_b), (V_LA, log_a), (V_NW, norm_w)):
                    for b in range(NB):
                        load(vec_rows[pos:pos + NL, b * DO:(b + 1) * DO], src)
                for b in range(NB):
                    load(lay_l[b * DO:(b + 1) * DO, :, 0:4], conv_w.rearrange("l c k -> c l k"))
                load(b2_all, b2_in.rearrange("e d -> (e d)")[None, :].to_broadcast([P, E * D]))
                sp.wait_ge(s_zero, 1)
                nat = work[:, RAW:RAW + 3 * NL * P].rearrange("p (m l i) -> p m l i", m=3, l=NL)
                for m, src in enumerate((gate_r_w, gate_i_w, out_w)):
                    for b in range(NB):
                        load(nat[b * DO:(b + 1) * DO, m, :, b * DO:(b + 1) * DO], src.rearrange("l o i -> o l i"))
                load(work[0:DO, RAW + 3 * NL * P:RAW + 3 * NL * P + D], down_w)
                upn = work[:, RAW + 3 * NL * P + D:RAW + 3 * NL * P + 2 * D].rearrange(
                    "p (k b i) -> p k b i", k=KD, b=NB)
                for b in range(NB):
                    load(upn[:, :, b, :], up_w.rearrange("(k p) i -> p k i", p=P))
                assert n_par[0] == N_PAR, n_par[0]

            for b in range(NB):
                sp.dma_start(rows_t[:, b * NC * TPC:b * NC * TPC + TPC, 0:D],
                             x_in[b * L:b * L + CH, :].rearrange("(j p) d -> p j d", p=P)).then_inc(s_x[0][b], 16)
            sp.dma_start(wr[:, :].rearrange("p (k e) -> p k e", k=KD),
                         router_w.rearrange("(k p) e -> p k e", p=P)).then_inc(s_rt, 16)
            sp.dma_start(rb_all[:, :], router_b[None, :].to_broadcast([P, E])).then_inc(s_rt, 16)
            for c in range(1, NC):
                for b in range(NB):
                    t0 = (b * NC + c) * TPC
                    sp.dma_start(rows_t[:, t0:t0 + TPC, 0:D],
                                 x_in[t0 * P:(t0 + TPC) * P, :].rearrange("(j p) d -> p j d", p=P)
                                 ).then_inc(s_x[0][c * NB + b], 16)
            def load_experts(experts):
                for e in experts:
                    sp.dma_start(w1[:, e * WE:(e + 1) * WE].rearrange("p (k f) -> p k f", k=KD),
                                 w1_in[e].rearrange("(k p) f -> p k f", p=P)).then_inc(s_w[e], 16)
                    sp.dma_start(w2[:, e * WE:(e + 1) * WE].rearrange("p (c d) -> p c d", c=FC),
                                 w2_in[e].rearrange("(c p) d -> p c d", p=P)).then_inc(s_w[e], 16)

            def report_experts(experts):
                for e in experts:
                    sp.wait_ge(s_w[e], 32)
                    sp.sem_inc(s_upto, FC)

            load_experts(range(0, EARLY // 2))
            load_parameters()
            load_experts(range(EARLY // 2, EARLY))
            sp.wait_ge(s_c2, 1)
            sp.dma_start(routed[E * REGION:E * REGION + P, :], fill[:, :]).then_inc(s_fill[0], 16)

            def feed_slots(m, phase):
                fill_regions(sp, phase, 0)
                sp.wait_ge(s_tab[phase], 1)
                sp.wait_ge(s_fill[phase], 16 * (E + (phase == 0)))
                sp.wait_ge(s_sc[phase], 16 * NT)

                def slot(t, i, s, reuse):
                    row = sp.value_load(tab_row[0:1, ds(t, 1)], min_val=0, max_val=E * REGION)
                    if reuse:
                        sp.wait_ge(m_s[m][s], i * 16)
                    sp.dma_start(pay[s], routed[ds(row, P), :]).then_inc(m_pay[m][s], 16)

                for s in range(RING):
                    slot(s, 0, s, False)
                if m == 0:
                    load_experts(range(EARLY, E))
                    report_experts(range(EARLY, E))
                with sp.Fori(1, NT // RING) as i:
                    for s in range(RING):
                        slot(i * RING + s, i, s, True)
                slot(NT, NT // RING, NT % RING, True)
                used = slots_used(sp)
                for t in range(NT + 1, SLOTS):
                    with sp.If(used > t - 1):
                        slot(t, t // RING, t % RING, True)

            def all_stored(m):
                counts = [sp.value_load(tab_stored[0:1, s:s + 1], min_val=16 * (NT // RING),
                                        max_val=16 * (SLOTS // RING + 1)) for s in range(RING)]
                for s in range(RING):
                    sp.wait_ge(m_s[m][s], counts[s])
                    sp.sem_inc(m_out[m])

            report_experts(range(EARLY))
            feed_slots(0, 0)
            all_stored(0)
            for c in range(NC):
                for b in range(NB):
                    t0 = (b * NC + c) * TPC
                    sp.dma_start(rows_t[:, t0:t0 + TPC, 0:D],
                                 x_mid[t0 * P:(t0 + TPC) * P, :].rearrange("(j p) d -> p j d", p=P)
                                 ).then_inc(s_x[1][c * NB + b], 16)
            sp.wait_ge(s_up, 2 * NB * NC)
            sp.dma_start(b2_all, b2_in.rearrange("e d -> (e d)")[None, :].to_broadcast([P, E * D])).then_inc(s_b2, 16)
            feed_slots(1, 2)
            all_stored(1)

        @block.gpsimd
        def _(pool):
            g = nc.gpsimd
            g.memset(ident[:, :], 0.0)
            g.memset(rec_t[:, 0:P], 1.0)
            g.memset(rec_t[:, P:2 * P], 1.0)
            g.iota(tab_b[:, 0:SLOTS], [[1, SLOTS]], base=0, channel_multiplier=0)
            g.iota(cnt_i[:, 0:E], [[-1, E]], base=E, channel_multiplier=0)
            g.iota(tab_fill[:, :], [[REGION, E]], base=0, channel_multiplier=0)
            g.iota(cnt_i[:, E:2 * E], [[REGION, E]], base=0, channel_multiplier=1)
            g.iota(rows_t[:, :, C_ID:C_ID + 1].bitcast(I32).rearrange("p t w -> p (t w)"), [[P, NT]], base=0,
                   channel_multiplier=1)
            g.memset(fill[:, 0:C_ID], 0.0)
            g.iota(fill[:, C_ID:C_ID + 1].bitcast(I32), [[0, 1]], base=T, channel_multiplier=1)
            g.memset(minus_half[:, :], -0.5)
            g.memset(eps_rms[:, :], RMS_EPS)
            g.memset(quarter[:, :], 0.25)
            g.memset(zero_e[:, :], 0.0)
            g.memset(carry[:, :], 1.0)
            g.memset(half_sel[:, :], 0.0)
            pool.drain()
            g.memset(carry[:, :].rearrange("p (e k) -> p e k", e=E)[:, :, 0:1], 0.0)
            for b in range(NB):
                g.memset(half_sel[b * DO:(b + 1) * DO, b:b + 1], 1.0)
                pool.drain()
            g.affine_select(out=ident[:, :], in_=ident[:, :], compare_op=ALU.not_equal, fill=1.0, base=0,
                            pattern=[[-1, P]], channel_multiplier=1)
            g.affine_select(out=rec_t[:, 0:P], in_=rec_t[:, 0:P], compare_op=ALU.is_ge, fill=0.0, base=-1,
                            pattern=[[1, P]], channel_multiplier=-1).then_inc(s_c1, 1)

            def powers(phase, c):
                pool.wait_ge(s_mv[phase], c + 1)
                g.tensor_tensor(inv_std[c % 2][:, :], var_eps[c % 2][:, :], minus_half[:, :], ALU.pow
                                ).then_inc(s_pow[phase], 1)

            def route(phase, c, sequences=range(NB)):
                pool.wait_ge(s_ds[phase], c + 1)
                for b in sequences:
                    for j in range(TPC):
                        t = (b * NC + c) * TPC + j
                        g.indirect_dma_start(
                            out=routed, out_offset=bass.IndirectOffsetOnAxis(ap=dest[:, t:t + 1], axis=0),
                            in_=rows[:, t * RW:(t + 1) * RW], in_offset=None,
                            bounds_check=E * REGION - 1, oob_is_err=False).then_inc(s_sc[phase], 16)

            def store_slots(m):
                target = x_mid if m == 0 else x_out
                last_token = pool.to_reg(T - 1)

                def slot(t, s):
                    pool.wait_ge(m_r[m], t + 1)
                    pool.sem_inc(m_go[m])
                    g.indirect_dma_start(
                        out=target, out_offset=bass.IndirectOffsetOnAxis(ap=pay[s][:, C_ID:C_ID + 1].bitcast(I32),
                                                                         axis=0),
                        in_=res[s % 2], in_offset=None, bounds_check=last_token, oob_is_err=False
                    ).then_inc(m_s[m][s], 16)

                with pool.Fori(0, NT // RING) as i:
                    for s in range(RING):
                        slot(i * RING + s, s)
                used = slots_used(pool)
                for t in range(NT, SLOTS):
                    with pool.If(used > t):
                        slot(t, t % RING)

            def routing(phase):
                for c in range(LEAD[phase]):
                    powers(phase, c)
                for c in range(NC):
                    route(phase, c, range(0, 1))
                    if c + LEAD[phase] < NC:
                        powers(phase, c + LEAD[phase])
                    route(phase, c, range(1, NB))

            routing(0)
            store_slots(0)
            for c in range(NC):
                powers(1, c)
            with pool.Fori(0, NL) as l:
                for c in range(NC):
                    pool.wait_ge(r_ti, l * NC + c + 1)
                    pool.wait_ge(r_in, l * NC + c + 1)
                    g.tensor_tensor(r_x_b[c], r_a_b[c], r_a_b[c], ALU.mult).then_inc(r_aa, 1)
            routing(2)
            store_slots(1)

        @block.vector
        def _(dve):
            v = nc.vector

            v.memset(work[:, RAW:RAW + 3 * NL * P], 0.0).then_inc(s_zero, 1)
            dve.wait_ge(s_c1, 1)
            v.tensor_copy(tri[:, :], rec_t[:, 0:P])
            v.tensor_copy(ones[:, :], rec_t[:, P:2 * P])
            v.tensor_copy(slot_no[:, :], tab_b[:, :])
            v.tensor_copy(e_desc[:, :], cnt_i[:, 0:E])
            v.tensor_copy(e_base[:, :], tab_fill[:, :])
            v.tensor_copy(e_fill[:, :], cnt_i[:, E:2 * E]).then_inc(s_c2, 1)

            def moments(phase, c):
                dve.drain()
                for b in range(NB):
                    for j in range(TPC):
                        jj = b * TPC + j
                        v.bn_stats(st[:, jj * 6:jj * 6 + 6], tile_of(c, b, j, 0, D))
                dve.drain()
                for jj in range(NJ):
                    v.bn_aggr(mv[c % 2][:, jj * 2:jj * 2 + 2], st[:, jj * 6:jj * 6 + 6])
                dve.drain()
                var = mv[c % 2][:, :].rearrange("p (j s) -> p j s", s=2)[:, :, 1]
                v.tensor_scalar(var_eps[c % 2][:, 0:NJ], var, 1.0, LN_EPS, ALU.mult, ALU.add)
                v.tensor_scalar(var_eps[c % 2][:, NJ:2 * NJ], var, 1.0 + LN_EPS, LN_EPS * LN_EPS, ALU.mult, ALU.add
                                ).then_inc(s_mv[phase], 1)

            def normalise(phase, c):
                dve.wait_ge(s_pow[phase], c + 1)
                lag = 1 if phase == 0 else 2
                if c >= lag:
                    dve.wait_ge(s_tr[phase], (c - lag + 1) * 4)
                m, r = mv[c % 2], inv_std[c % 2]
                for b in range(NB):
                    for j in range(TPC):
                        jj = b * TPC + j
                        v.tensor_scalar(xn[phase][c % 2][:, jj, :], tile_of(c, b, j, 0, D), m[:, 2 * jj:2 * jj + 1],
                                        r[:, jj:jj + 1], ALU.subtract, ALU.mult)
                v.tensor_copy(column_of(c, C_MEAN), m[:, :].rearrange("p (b j s) -> p b j s", b=NB, s=2)[:, :, :, 0])
                v.tensor_copy(column_of(c, C_RS), r[:, NJ:2 * NJ].rearrange("p (b j) -> p b j", b=NB)
                              ).then_inc(s_xn[phase], 1)

            def jx(a):
                return a[:, :].rearrange("p (j e) -> p j e", e=E)

            def per_e(a):
                return a[:, None, :].to_broadcast([P, NJ, E])

            def per_j(a):
                return a[:, :, None].to_broadcast([P, NJ, E])

            def choose(phase, c):
                dve.wait_ge(s_lg[phase], c + 1)
                v.tensor_tensor(jx(lgt), bank[4 + c % 2][:, 0:NJ * E].rearrange("p (j e) -> p j e", e=E),
                                per_e(rb_all), ALU.add)
                dve.drain()
                v.tensor_reduce(top[:, :], jx(lgt), AX.X, ALU.max)
                dve.drain()
                v.tensor_tensor(jx(below), jx(lgt), per_j(top), ALU.subtract).then_inc(s_ex[phase], 1)
                v.tensor_tensor(jx(hit), jx(lgt), per_j(top), ALU.is_equal)
                dve.drain()
                v.tensor_tensor(jx(hit), jx(hit), per_e(e_desc), ALU.mult)
                dve.drain()
                v.tensor_reduce(first[:, :], jx(hit), AX.X, ALU.max)
                dve.drain()
                v.tensor_tensor(onehot_j, per_j(first), per_e(e_desc), ALU.is_equal)
                dve.drain()
                v.tensor_tensor_scan(sums[:, :], carry[:, :], chosen[:, :], 0.0, ALU.mult, ALU.add
                                     ).then_inc(s_oh[phase], 1)

            def place(phase, c):
                dve.wait_ge(s_exd[phase], c + 1)
                v.tensor_reduce(den[:, :], jx(expo), AX.X, ALU.add)
                dve.drain()
                v.reciprocal(top[:, :], den[:, :])
                dve.drain()
                v.tensor_scalar(column_of(c, C_GATE), top[:, :].rearrange("p (b j) -> p b j", b=NB), 0.5, None, ALU.mult)
                dve.wait_ge(s_rk[phase], c + 1)
                v.tensor_copy(seen, sums_t[:, :, NJ:NJ + 1])
                v.tensor_tensor(jx(rank), bank[4 + c % 2][:, NJ * E:2 * NJ * E].rearrange("p (e j) -> p j e", e=E),
                                per_e(e_base), ALU.add)
                dve.drain()
                v.tensor_tensor(jx(rank), jx(rank), onehot_j, ALU.mult)
                dve.drain()
                v.tensor_reduce(dest_f[:, :], jx(rank), AX.X, ALU.add)
                dve.drain()
                d = dest[:, :].rearrange("p (b c j) -> p b c j", b=NB, c=NC)[:, :, ds(c, 1), :].rearrange(
                    "p b o j -> p b (o j)")
                v.tensor_copy(d, dest_f[:, :].rearrange("p (b j) -> p b j", b=NB)).then_inc(s_ds[phase], 1)

            def tables(phase):
                dve.wait_ge(s_cnt[phase], 1)
                v.tensor_copy(cnt[:, :], bank[6][:, 0:E])
                v.tensor_scalar(cnt_i[:, 0:E], bank[6][:, 0:E], float(P - 1), None, ALU.add)
                dve.drain()
                v.tensor_tensor(tab_fill[:, :], cnt[:, :], e_base[:, :], ALU.add).then_inc(s_end[phase], 1)
                v.tensor_scalar(cnt_i[:, E:2 * E], cnt_i[:, 0:E], P.bit_length() - 1, None, ALU.logical_shift_right)
                dve.drain()
                v.tensor_copy(tiles_of[:, :], cnt_i[:, E:2 * E])
                dve.drain()
                v.tensor_tensor_scan(tile_end[:, :], tiles_of[:, :], zero_e[:, :], 0.0, ALU.add, ALU.add)
                v.tensor_scalar(skip[:, :], tiles_of[:, :], -float(P), float(REGION), ALU.mult, ALU.add)
                dve.drain()
                ps = past.rearrange("p (t e) -> p t e", e=E)
                jp = jump.rearrange("p (t e) -> p t e", e=E)
                v.tensor_tensor(ps, slot_no[:, :, None].to_broadcast([P, SLOTS, E]),
                                tile_end[:, None, :].to_broadcast([P, SLOTS, E]), ALU.is_ge)
                dve.drain()
                v.tensor_reduce(slot_e[:, :], ps, AX.X, ALU.add)
                v.tensor_tensor(jp, ps, skip[:, None, :].to_broadcast([P, SLOTS, E]), ALU.mult)
                dve.drain()
                v.tensor_reduce(slot_r[:, :], jp, AX.X, ALU.add)
                v.tensor_copy(tab_used[:, :], tile_end[:, E - 1:E])
                for s in range(RING):
                    v.tensor_scalar(uses_i[:, s:s + 1], tile_end[:, E - 1:E], float(RING - 1 - s), None, ALU.add)
                dve.drain()
                v.tensor_scalar(uses_i[:, :], uses_i[:, :], RING.bit_length() - 1, None, ALU.logical_shift_right)
                dve.drain()
                v.tensor_copy(uses[:, :], uses_i[:, :])
                dve.drain()
                v.tensor_scalar(tab_stored[:, :], uses[:, :], 16.0, None, ALU.mult)
                v.tensor_scalar(tab_b[:, :], slot_e[:, :], float(E - 1), float(FC), ALU.min, ALU.mult)
                dve.drain()
                v.scalar_tensor_tensor(out=slot_r[:, :], in0=slot_no[:, :], scalar=float(P), in1=slot_r[:, :],
                                       op0=ALU.mult, op1=ALU.add)
                dve.drain()
                v.tensor_scalar(tab_row[:, :], slot_r[:, :], float(E * REGION), None, ALU.min).then_inc(s_tab[phase], 1)
                dve.drain()

            def routing(phase, before):
                v.memset(seen, 0.0)
                for c in range(LEAD[phase]):
                    before(c)
                    moments(phase, c)
                    if c:
                        normalise(phase, c - 1)
                if phase == 0:
                    dve.wait_ge(s_rt, 32)
                else:
                    normalise(phase, 1)
                for c in range(NC):
                    choose(phase, c)
                    if phase == 0 and c + 2 < NC:
                        normalise(phase, c + 2)
                    place(phase, c)
                    if c + LEAD[phase] < NC:
                        before(c + LEAD[phase])
                        moments(phase, c + LEAD[phase])
                        if phase == 2:
                            normalise(phase, c + 2)
                dve.drain()
                v.tensor_copy(top[:, 0:1], dest_f[:, 0:1]).then_inc(s_seen[phase], 1)
                tables(phase)

            def slots(m):
                def norm(t, i, s):
                    dve.wait_ge(m_pay[m][s], i * 16 + 16)
                    p = pay[s]
                    v.tensor_scalar(mn[s % 2], p[:, 0:D], p[:, C_MEAN:C_MEAN + 1], p[:, C_RS:C_RS + 1],
                                    ALU.subtract, ALU.mult).then_inc(m_xn[m], 1)

                def activate(t, s):
                    eb = dve.value_load(tab_b[0:1, ds(t, 1)], min_val=0, max_val=(E - 1) * FC)
                    for c in range(FC):
                        if c % 4 == 0:
                            dve.wait_ge(m_ht[m], t * 2 + c // 4 + 1)
                        last = v.tensor_scalar(act_t[s % 2][:, c * P:(c + 1) * P],
                                               bank[3 + c // 4][:, c % 4 * P:(c % 4 + 1) * P],
                                               vec[:, ds(eb + c, 1)], 0.0, ALU.add, ALU.max)
                    last.then_inc(m_a[m], 1)

                def finish(t, s, stored):
                    eb = dve.value_load(tab_b[0:1, ds(t, 1)], min_val=0, max_val=(E - 1) * FC)
                    dve.wait_ge(m_y[m], t + 1)
                    v.tensor_tensor(y_b, bank[5][:, 0:D], b2_all[:, ds(eb * (D // FC), D)], ALU.add)
                    dve.drain()
                    if stored is not None:
                        dve.wait_ge(m_s[m][(s + 2) % RING], stored)
                    v.scalar_tensor_tensor(out=res[s % 2], in0=y_b, scalar=pay[s][:, C_GATE:C_GATE + 1],
                                           in1=pay[s][:, 0:D], op0=ALU.mult, op1=ALU.add).then_inc(m_r[m], 1)

                def step(t, i, s, more=True, stored=True):
                    if more:
                        norm(t + 1, i + (s + 1) // RING, (s + 1) % RING)
                    s1, i1 = (s - 1) % RING, i - (s == 0)
                    finish(t - 1, s1, (i1 * 16 + 16 if s1 >= 2 else i1 * 16) if stored else None)
                    activate(t, s)

                if m == 1:
                    dve.wait_ge(s_b2, 16)
                norm(0, 0, 0)
                norm(1, 0, 1)
                activate(0, 0)
                step(1, 0, 1, stored=False)
                step(2, 0, 2, stored=False)
                step(3, 0, 3)
                with dve.Fori(1, NT // RING) as i:
                    for s in range(RING):
                        step(i * RING + s, i, s)
                used = slots_used(dve)
                for t in range(NT, SLOTS):
                    with dve.If(used > t):
                        step(t, t // RING, t % RING, more=t + 1 < SLOTS)
                for t in range(NT - 1, SLOTS):
                    with dve.If(used == t + 1):
                        finish(t, t % RING, (t - 2) // RING * 16 + 16)

            def x_arrives(c):
                for b in range(NB):
                    dve.wait_ge(s_x[0][c * NB + b], 16)

            def parameters():
                dve.wait_ge(s_tpe, 1)
                la = vec[:, V_LA:V_LA + NL]
                a0, a1, a2, a3 = (hit[:, 8 * i:8 * i + NL] for i in range(4))
                v.tensor_copy(lay_l[:, :, U_CB], vec[:, V_CB:V_CB + NL])
                v.tensor_copy(lay_l[:, :, U_NW], vec[:, V_NW:V_NW + NL])
                v.tensor_scalar(lay_l[:, :, U_RB], vec[:, V_RB:V_RB + NL], 0.5, None, ALU.mult)
                v.tensor_scalar(lay_l[:, :, U_IB], vec[:, V_IB:V_IB + NL], 0.5, None, ALU.mult)
                v.scalar_tensor_tensor(out=a0, in0=la, scalar=-1.0, in1=la, op0=ALU.mult, op1=ALU.max).then_inc(s_absla, 1)
                dve.wait_ge(s_expla, 1)
                v.tensor_scalar(a2, a1, 2.0, None, ALU.add)
                dve.drain()
                v.reciprocal(a3, a2)
                dve.drain()
                v.tensor_tensor(a1, a1, a3, ALU.mult)
                dve.drain()
                v.tensor_tensor(a2, a1, a1, ALU.mult)
                dve.drain()
                v.tensor_scalar(a3, a2, 1.0 / (2 * LOG1P_TERMS + 1), None, ALU.mult)
                for k in range(LOG1P_TERMS - 1, 0, -1):
                    dve.drain()
                    v.scalar_tensor_tensor(out=a3, in0=a3, scalar=1.0 / (2 * k + 1), in1=a2, op0=ALU.add, op1=ALU.mult)
                dve.drain()
                v.scalar_tensor_tensor(out=a3, in0=a3, scalar=1.0, in1=a1, op0=ALU.add, op1=ALU.mult)
                v.tensor_scalar(a0, la, 0.0, 4.0, ALU.min, ALU.mult)
                dve.drain()
                v.scalar_tensor_tensor(out=lay_l[:, :, U_LS], in0=a3, scalar=-8.0, in1=a0, op0=ALU.mult, op1=ALU.add
                                       ).then_inc(s_lsd, 1)

            routing(0, x_arrives)
            parameters()
            slots(0)

            def mid_arrives(c):
                for b in range(NB):
                    dve.wait_ge(s_x[1][c * NB + b], 16)

            dve.wait_ge(m_end, 1)
            mid_arrives(0)
            moments(1, 0)
            for c in range(NC):
                if c + 1 < NC:
                    mid_arrives(c + 1)
                    moments(1, c + 1)
                normalise(1, c)

            dve.wait_ge(s_seq, NC)
            v.memset(seq[:, 0:3], 0.0).then_inc(r_xx, NC)
            v.memset(rms_i[:, :], 0.0).then_inc(r_h, 1)
            dve.drain()

            def convolve(l, c):
                xc = r_x_b[c]
                dve.wait_ge(r_c0, l * NC + c + 1)
                for k in range(2, -1, -1):
                    last = v.scalar_tensor_tensor(out=xc, in0=seq[:, c * CH + k:c * CH + k + CH],
                                                  scalar=cur[:, k:k + 1], in1=xc, op0=ALU.mult, op1=ALU.add)
                    if k:
                        dve.drain()
                last.then_inc(r_xc, 1)

            def gate_input(l, c):
                dve.wait_ge(r_ti, l * NC + c + 1)
                v.scalar_tensor_tensor(out=r_ti_b[c], in0=r_ti_b[c], scalar=1.0, in1=r_x_b[c],
                                       op0=ALU.add, op1=ALU.mult).then_inc(r_in, 1)

            def clamp(l, c):
                dve.wait_ge(r_aa, l * NC + c + 1)
                v.tensor_scalar(r_x_b[c], r_x_b[c], 1.0, None, ALU.min).then_inc(r_q, 1)

            def scan(l, c):
                dve.wait_ge(r_gt, l * NC + c + 1)
                v.tensor_tensor(r_x_b[c], r_x_b[c], r_ti_b[c], ALU.mult)
                dve.drain()
                prev = 0.0 if c == 0 else r_a_b[c - 1][:, CH - 1:CH]
                v.tensor_tensor_scan(r_a_b[c], r_a_b[c], r_x_b[c], prev, ALU.mult, ALU.add).then_inc(r_h, 1)

            def inverse(l, h):
                dve.wait_ge(r_sr, 2 * l + h + 1)
                half = slice(h * NH, (h + 1) * NH)
                v.reciprocal(rms_i[:, half], rms_s[:, half])
                dve.drain()
                for c in range(h * HC, (h + 1) * HC):
                    v.tensor_copy(r_a_b[c].rearrange("p (g n) -> p g n", n=DO),
                                  rms_i[:, c * TPC * NB:(c + 1) * TPC * NB, None].to_broadcast([P, TPC * NB, DO])
                                  ).then_inc(r_si, 1)

            def rescale(l, c):
                dve.wait_ge(r_rb, l * NC + c + 1)
                v.tensor_tensor(seq[:, 3 + c * CH:3 + (c + 1) * CH], r_ti_b[c], bank[c][:, :], ALU.mult
                                ).then_inc(r_xx, 1)

            with dve.Fori(0, NL) as l:
                for c in range(AHEAD):
                    convolve(l, c)
                for c in range(NC):
                    gate_input(l, c)
                    if c + AHEAD < NC:
                        convolve(l, c + AHEAD)
                clamp(l, 0)
                for c in range(NC):
                    if c + 1 < NC:
                        clamp(l, c + 1)
                    scan(l, c)
                for h in range(2):
                    inverse(l, h)
                    for c in range(h * HC, (h + 1) * HC):
                        rescale(l, c)
                dve.drain()

            def recurrence_arrives(c):
                for b in range(NB):
                    for hh in range(2):
                        n = (c * NB + b) * 2 + hh
                        dve.wait_ge(s_up, n + 1)
                        r = rows_t[:, (b * NC + c) * TPC + 2 * hh:(b * NC + c) * TPC + 2 * hh + 2, 0:D]
                        v.tensor_tensor(r, r, bank[7 if hh else 6][:, :].rearrange("p (j d) -> p j d", d=D), ALU.add
                                        ).then_inc(s_add, 1)
                dve.drain()

            routing(2, recurrence_arrives)
            slots(1)

        @block.scalar
        def _(act):
            a = nc.scalar
            def parameters():
                act.wait_ge(s_tp, 1)
                a.activation(vec[:, :], bank[0][:, 0:NV], ACT.Copy).then_inc(s_tpe, 1)
                for m in range(3):
                    a.activation(rec_t[:, m * NL * P:(m + 1) * NL * P], bank[1 + m][:, 0:NL * P], ACT.Copy)
                a.activation(down_t[:, :], bank[4][:, 0:KD * DO], ACT.Copy)
                a.activation(up_t[:, :], bank[5][:, 0:D], ACT.Copy).then_inc(s_tpe, 1)
                act.wait_ge(s_absla, 1)
                a.activation(hit[:, 8:8 + NL], hit[:, 0:NL], ACT.Exp, scale=-1.0).then_inc(s_expla, 1)

            def keep(phase, c, guard):
                for n in range(NB * KD):
                    act.wait_ge(s_tr[phase], c * 4 + n + 1)
                    if n == 0 and guard:
                        act.wait_ge(s_lg[phase] if phase != 1 else s_dn, c)
                    a.activation(xn_t[:, n // KD, n % KD, :], bank[n][:, :], ACT.Copy).then_inc(s_te[phase], 1)

            def exponentials(phase, c):
                act.wait_ge(s_ex[phase], c + 1)
                a.activation(expo[:, :], below[:, :], ACT.Exp).then_inc(s_exd[phase], 1)

            def routing(phase):
                keep(phase, 0, False)
                with act.Fori(1, NC) as c:
                    keep(phase, c, True)
                    exponentials(phase, c - 1)
                exponentials(phase, NC - 1)

            def slots(m):
                def affine(t, s):
                    act.wait_ge(m_xt[m], t + 1)
                    for k in range(KD):
                        last = a.activation(mn_t[s % 2][:, k * P:(k + 1) * P], bank[0][:, k * P:(k + 1) * P], ACT.Identity,
                                            scale=vec[:, V_G + k:V_G + k + 1], bias=vec[:, V_B + k:V_B + k + 1])
                    last.then_inc(m_xk[m], 1)

                def hidden(t):
                    for n in range(2):
                        act.wait_ge(m_h[m], t * 2 + n + 1)
                        a.activation(hid[:, n * 512:(n + 1) * 512], bank[1 + n][:, :], ACT.Copy).then_inc(m_hk[m], 1)

                affine(0, 0)
                hidden(0)
                affine(1, 1)
                with act.Fori(0, (NT - 2) // 2) as i:
                    for s in range(2):
                        hidden(i * 2 + 1 + s)
                        affine(i * 2 + 2 + s, s)
                hidden(NT - 1)
                affine(NT, NT % 2)
                used = slots_used(act)
                for t in range(NT, SLOTS):
                    with act.If(used > t):
                        hidden(t)
                        if t + 1 < SLOTS:
                            affine(t + 1, (t + 1) % 2)

            routing(0)
            fill_regions(act, 0, 1)
            parameters()
            slots(0)
            act.drain()
            a.activation(rms_s[:, 0:1], quarter[:, :], ACT.Copy).then_inc(m_end, 1)
            for c in range(NC):
                keep(1, c, c > 0)
                act.wait_ge(s_dn, c + 1)
                a.activation(seq[:, 3 + c * CH:3 + (c + 1) * CH], bank[4][:, :], ACT.Copy).then_inc(s_seq, 1)
            act.wait_ge(s_lsd, 1)
            act.drain()

            with act.Fori(0, NL) as l:
                for m in range(3):
                    a.activation(rec_cur[:, m * P:(m + 1) * P], rec_t[:, ds(l * P + m * NL * P, P)], ACT.Copy
                                 ).then_inc(r_w, 1)
                a.activation(cur[:, :], lay[:, ds(l * NU, NU)], ACT.Copy)
                act.drain()

                def tap(c):
                    act.wait_ge(r_xx, l * NC + c + 1)
                    a.activation(r_x_b[c], seq[:, 3 + c * CH:3 + (c + 1) * CH], ACT.Identity,
                                 scale=cur[:, 3:4], bias=cur[:, U_CB:U_CB + 1]).then_inc(r_c0, 1)

                def gates(c):
                    act.wait_ge(r_g, (l * NC + c) * 2 + 2)
                    a.activation(r_a_b[c], bank[2 * c][:, :], ACT.Tanh, scale=0.5, bias=cur[:, U_RB:U_RB + 1])
                    a.activation(r_ti_b[c], bank[2 * c + 1][:, :], ACT.Tanh, scale=0.5,
                                 bias=cur[:, U_IB:U_IB + 1])
                    act.drain()
                    a.activation(r_a_b[c], r_a_b[c], ACT.Exp, scale=cur[:, U_LS:U_LS + 1],
                                 bias=cur[:, U_LS:U_LS + 1]).then_inc(r_ti, 1)

                def root(c):
                    act.wait_ge(r_q, l * NC + c + 1)
                    a.activation(r_x_b[c], r_x_b[c], ACT.Sqrt, scale=-0.25, bias=quarter[:, :]
                                 ).then_inc(r_gt, 1)

                def squares(c):
                    act.wait_ge(r_y, l * NC + c + 1)
                    a.activation(r_ti_b[c], bank[4 + c % 3][:, :], ACT.Copy, scale=cur[:, U_NW:U_NW + 1])
                    a.activation(r_x_b[c], bank[4 + c % 3][:, :], ACT.Square).then_inc(r_yk, 1)

                for c in range(AHEAD):
                    tap(c)
                for c in range(NC):
                    gates(c)
                    if c + AHEAD < NC:
                        tap(c + AHEAD)
                root(0)
                for c in range(NC):
                    if c + 1 < NC:
                        root(c + 1)
                    squares(c)
                    if c >= NC - 2:
                        h = c - (NC - 2)
                        act.wait_ge(r_ss, l * NC + (h + 1) * HC)
                        a.activation(rms_s[:, h * NH:(h + 1) * NH], sums_of_squares[h], ACT.Sqrt, scale=1.0 / DO,
                                     bias=eps_rms[:, :]).then_inc(r_sr, 1)
            routing(2)
            fill_regions(act, 2, 1)
            slots(1)

        @block.tensor
        def _(pe):
            t = nc.tensor
            def parameters():
                pe.wait_ge(s_par, 16 * N_PAR)
                t.transpose(bank[0][:, 0:NV], vec_rows, ident[0:NV, 0:NV])
                for m in range(3):
                    for l in range(NL):
                        t.transpose(bank[1 + m][:, l * P:(l + 1) * P],
                                    work[:, RAW + (m * NL + l) * P:RAW + (m * NL + l + 1) * P],
                                    ident[:, :])
                q = RAW + 3 * NL * P
                for k in range(KD):
                    t.transpose(bank[4][:, k * DO:(k + 1) * DO], work[0:DO, q + k * P:q + (k + 1) * P], ident[0:DO, 0:DO])
                for k in range(KD):
                    last = t.transpose(bank[5][:, k * P:(k + 1) * P], work[:, q + D + k * P:q + D + (k + 1) * P],
                                       ident[:, :])
                last.then_inc(s_tp, 1)
                pe.wait_ge(s_tpe, 2)

            def transposes(phase, c, first):
                pe.wait_ge(s_xn[phase], c + 1)
                for b in range(NB):
                    for k in range(KD):
                        n = b * KD + k
                        if not first:
                            pe.wait_ge(s_te[phase], (c - 1) * 4 + n + 1)
                        for j in range(TPC):
                            last = t.transpose(bank[n][:, j * P:(j + 1) * P],
                                               xn[phase][c % 2][:, b * TPC + j, k * P:(k + 1) * P], ident[:, :])
                        last.then_inc(s_tr[phase], 1)

            def logits(phase, c):
                pe.wait_ge(s_te[phase], c * 4 + 4)
                if c >= 2:
                    pe.wait_ge(s_ds[phase], c - 1)
                for b in range(NB):
                    for j in range(TPC):
                        o = (b * TPC + j) * E
                        for k in range(KD):
                            last = t.matmul(bank[4 + c % 2][:, o:o + E], xn_t[:, b, k, j * P:(j + 1) * P],
                                            wr[:, k * E:(k + 1) * E], start=k == 0, stop=k == KD - 1)
                last.then_inc(s_lg[phase], 1)

            def ranks(phase, c):
                pe.wait_ge(s_oh[phase], c + 1)
                o3 = bank[4 + c % 2][:, NJ * E:2 * NJ * E]
                o3 = o3.rearrange("p (e j) -> p e j", e=E)
                t.matmul(o3, tri[:, :], onehot, start=True, stop=False)
                t.matmul(o3, ones[:, :], sums_t[:, :, 0:NJ], start=False, stop=True).then_inc(s_rk[phase], 1)

            def up(c):
                pe.wait_ge(r_xx, NL * NC + c + 1)
                for b in range(NB):
                    for hh in range(2):
                        n = (c * NB + b) * 2 + hh
                        if n >= 2:
                            pe.wait_ge(s_add, n - 1)
                        for j in range(2):
                            jj = 2 * hh + j
                            last = t.matmul(bank[7 if hh else 6][:, j * D:(j + 1) * D],
                                            seq[b * DO:(b + 1) * DO, 3 + c * CH + jj * P:3 + c * CH + (jj + 1) * P],
                                            up_t[b * DO:(b + 1) * DO, :], start=True, stop=True)
                        last.then_inc(s_up, 1)

            def routing(phase):
                if phase == 2:
                    up(0)
                    up(1)
                transposes(phase, 0, True)
                logits(phase, 0)
                transposes(phase, 1, False)
                for c in range(NC):
                    ranks(phase, c)
                    if phase == 0:
                        if c + 1 < NC:
                            logits(phase, c + 1)
                        if c + 2 < NC:
                            transposes(phase, c + 2, False)
                    else:
                        if c + 2 < NC:
                            up(c + 2)
                        if c + 1 < NC:
                            logits(phase, c + 1)
                        if c + 2 < NC:
                            transposes(phase, c + 2, False)
                pe.wait_ge(s_seen[phase], 1)
                t.matmul(bank[6][:, 0:E].rearrange("p (e o) -> p e o", o=1), ones[:, :], seen, start=True, stop=True
                         ).then_inc(s_cnt[phase], 1)

            def slots(m):
                def turn_input(i, s, first=False):
                    pe.wait_ge(m_xn[m], i + 1)
                    if not first:
                        pe.wait_ge(m_xk[m], i)
                    for k in range(KD):
                        last = t.transpose(bank[0][:, k * P:(k + 1) * P], mn[s][:, k * P:(k + 1) * P], ident[:, :])
                    last.then_inc(m_xt[m], 1)

                def expert_of(i):
                    return pe.value_load(tab_b[0:1, ds(i, 1)], min_val=0, max_val=(E - 1) * FC)

                def hidden(i, s, eb, first=False):
                    pe.wait_ge(m_xk[m], i + 1)
                    if m == 0:
                        pe.wait_ge(s_upto, eb + FC)
                    for n in range(2):
                        if not first:
                            pe.wait_ge(m_hk[m], (i - 1) * 2 + n + 1)
                        for k in range(KD):
                            last = t.matmul(bank[1 + n][:, :], mn_t[s][:, k * P:(k + 1) * P],
                                            w1[:, ds(eb * (WE // FC) + (k * F + n * 512), 512)], start=k == 0, stop=k == KD - 1)
                        last.then_inc(m_h[m], 1)

                def turn_hidden(i, first=False):
                    for n in range(2):
                        pe.wait_ge(m_hk[m], i * 2 + n + 1)
                        if not first:
                            pe.wait_ge(m_a[m], i)
                        for j in range(4):
                            last = t.transpose(bank[3 + n][:, j * P:(j + 1) * P],
                                               hid[:, (4 * n + j) * P:(4 * n + j + 1) * P], ident[:, :])
                        last.then_inc(m_ht[m], 1)

                def expert_out(i, s, eb, first=False):
                    pe.wait_ge(m_a[m], i + 1)
                    if not first:
                        pe.wait_ge(m_r[m], i)
                    for c in range(FC):
                        last = t.matmul(bank[5][:, 0:D], act_t[s][:, c * P:(c + 1) * P],
                                        w2[:, ds(eb * (WE // FC) + c * D, D)], start=c == 0, stop=c == FC - 1)
                    last.then_inc(m_y[m], 1)

                def step(i, s, eb_before, first=False, more=True):
                    eb = expert_of(i)
                    if eb_before is None:
                        eb_before = expert_of(i - 1)
                    hidden(i, s, eb)
                    if more:
                        turn_input(i + 1, 1 - s)
                    expert_out(i - 1, 1 - s, eb_before, first)
                    turn_hidden(i)
                    return eb

                pe.wait_ge(s_tab[0 if m == 0 else 2], 1)
                turn_input(0, 0, True)
                eb = expert_of(0)
                hidden(0, 0, eb, True)
                turn_input(1, 1)
                turn_hidden(0, True)
                step(1, 1, eb, True)
                with pe.Fori(0, (NT - 2) // 2) as i:
                    eb = step(i * 2 + 2, 0, None)
                    step(i * 2 + 3, 1, eb)
                used = slots_used(pe)
                for i in range(NT, SLOTS):
                    with pe.If(used > i):
                        step(i, i % 2, None, more=i + 1 < SLOTS)
                for i in range(NT - 1, SLOTS):
                    with pe.If(used == i + 1):
                        expert_out(i, i % 2, expert_of(i))

            pe.wait_ge(s_c2, 1)
            pe.wait_ge(s_rt, 32)
            routing(0)
            parameters()
            slots(0)
            for c in range(NC):
                transposes(1, c, c == 0)
                pe.wait_ge(s_te[1], c * 4 + 4)
                if c:
                    pe.wait_ge(s_seq, c)
                for b in range(NB):
                    for k in range(KD):
                        last = t.matmul(bank[4][b * DO:(b + 1) * DO, :], down_t[:, k * DO:(k + 1) * DO],
                                        xn_t[:, b, k, :], start=k == 0, stop=k == KD - 1)
                last.then_inc(s_dn, 1)

            with pe.Fori(0, NL) as l:
                pe.wait_ge(r_w, l * 3 + 3)

                def gates(c):
                    pe.wait_ge(r_xc, l * NC + c + 1)
                    for m in range(2):
                        t.matmul(bank[2 * c + m][:, :], rec_cur[:, m * P:(m + 1) * P], r_x_b[c],
                                 start=True, stop=True).then_inc(r_g, 1)

                def project(c):
                    pe.wait_ge(r_h, l * NC + c + 2)
                    if c >= 3:
                        pe.wait_ge(r_yk, l * NC + c - 2)
                    t.matmul(bank[4 + c % 3][:, :], rec_cur[:, 2 * P:3 * P], r_a_b[c], start=True, stop=True
                             ).then_inc(r_y, 1)

                def norms(c):
                    pe.wait_ge(r_yk, l * NC + c + 1)
                    for j in range(TPC):
                        o = (c % HC * TPC + j) * NB
                        last = t.matmul(sums_of_squares[c // HC][:, o:o + NB], r_x_b[c][:, j * P:(j + 1) * P],
                                        half_sel[:, :], start=True, stop=True)
                    last.then_inc(r_ss, 1)

                def spread(c):
                    pe.wait_ge(r_si, l * NC + c + 1)
                    for j in range(TPC):
                        last = t.transpose(bank[c][:, j * P:(j + 1) * P], r_a_b[c][:, j * P:(j + 1) * P], ident[:, :])
                    last.then_inc(r_rb, 1)

                for c in range(NC):
                    gates(c)
                project(0)
                for c in range(NC):
                    if c + 1 < NC:
                        project(c + 1)
                    if c == NC - 1:
                        for cc in range(HC):
                            spread(cc)
                    norms(c)
                for c in range(HC, NC):
                    spread(c)
            routing(2)
            slots(1)


_INS = ["L0_attn_h", "L0_attn_down_w", "L0_attn_up_w", "L0_attn_conv_w", "L0_attn_conv_b", "L0_attn_Wr_w",
        "L0_attn_Wr_b", "L0_attn_Wi_w", "L0_attn_Wi_b", "L0_attn_log_a", "L0_attn_out_w", "L0_attn_norm_w",
        "L0_ffn_Wr", "L0_ffn_br", "L0_ffn_ln_g", "L0_ffn_ln_b", "L0_ffn_W1", "L0_ffn_b1", "L0_ffn_W2", "L0_ffn_b2"]


def kernel(**inputs):
    import numpy as _np
    import concourse.bacc as _bacc
    from concourse import mybir as _mybir
    from concourse.bass_utils import run_bass_kernel_spmd as _run

    nc = _bacc.Bacc("TRN2", target_bir_lowering=False, num_devices=1)
    arrays, args = {}, []
    for name in _INS:
        a = _np.ascontiguousarray(inputs[name])
        arrays[f"in_{name}"] = a
        args.append(nc.dram_tensor(f"in_{name}", a.shape, _mybir.dt.from_np(a.dtype), kind="ExternalInput").ap())
    x = arrays["in_L0_attn_h"]
    args.append(nc.dram_tensor("out_x", x.shape, _mybir.dt.from_np(x.dtype), kind="ExternalOutput").ap())
    macaron_block(nc, *args)
    return _run(nc, [arrays], core_ids=[0]).results[0]["out_x"]
```
